# Optimizing a Trainium2 kernel written in Bass

```python
import numpy as np
import jax
import jax.numpy as jnp

def _softmax(x, axis=-1):
    return jax.nn.softmax(x, axis=axis)

def _gelu(x):
    return jax.nn.gelu(x, approximate=True)

def _silu(x):
    return jax.nn.silu(x)

def _sigmoid(x):
    return jax.nn.sigmoid(x)

def _layernorm(x, axis=-1, eps=1e-05):
    m = jnp.mean(x, axis=axis, keepdims=True)
    v = jnp.var(x, axis=axis, keepdims=True)
    return (x - m) / jnp.sqrt(v + eps)

def _scatter_add(tgt, idx, src, axis=0):
    return tgt.at[idx].add(src)

def _segment_sum(src, seg, n):
    return jax.ops.segment_sum(src, seg, n)
kernel_name = 'mk_macaron_d2_jaxref_r4_281ae0'

def setup_inputs(seed: int=0):
    np.random.seed(seed)
    _w = jnp.asarray

    def _L0_attn_setup():
        import jax, jax.numpy as jnp
        import numpy as np
        DIL = (1, 2, 4)
        SEG = (128, 128, 128)
        H = 16
        D = 256
        B, L = (2, 2048)

        def _mha(x, Wqkv, bqkv, Wo, bo):
            lead = x.shape[:-2]
            S = x.shape[-2]
            hd = D // H
            qkv = x @ Wqkv.T + bqkv
            q, k, v = jnp.split(qkv, 3, axis=-1)
            q = q.reshape(*lead, S, H, hd)
            k = k.reshape(*lead, S, H, hd)
            v = v.reshape(*lead, S, H, hd)
            scale = 1.0 / np.float32(np.sqrt(hd))
            scores = jnp.einsum('...qhd,...khd->...hqk', q, k) * scale
            a = jax.nn.softmax(scores, axis=-1)
            o = jnp.einsum('...hqk,...khd->...qhd', a, v).reshape(*lead, S, D)
            return o @ Wo.T + bo
        key = jax.random.key(seed)
        ks = jax.random.split(key, 5)
        n = len(DIL)
        x = jax.random.normal(ks[0], (B, L, D), dtype=jnp.float32)
        Wqkv = 0.02 * jax.random.normal(ks[1], (n, 3 * D, D), dtype=jnp.float32)
        bqkv = jnp.zeros((n, 3 * D), dtype=jnp.float32)
        Wout = 0.02 * jax.random.normal(ks[2], (n, D, D), dtype=jnp.float32)
        bout = jnp.zeros((n, D), dtype=jnp.float32)
        return {'x': x, 'Wqkv': Wqkv, 'bqkv': bqkv, 'Wout': Wout, 'bout': bout}
    _L0_attn_in = _L0_attn_setup()

    def _L0_ffn_setup():
        import jax, jax.numpy as jnp
        import numpy as np
        B, T, H = (2, 512, 256)
        I = 1024
        HEADS = 4
        RET = 128
        NUM_EXPERTS = 1024
        NUM_KEYS = 64
        K = 8
        key = jax.random.key(seed)
        ks = jax.random.split(key, 7)
        return {'hidden_states': jax.random.normal(ks[0], (B, T, H), jnp.float32), 'W_up': jax.random.normal(ks[1], (I, H), jnp.float32) * 0.02, 'W_down': jax.random.normal(ks[2], (H, I), jnp.float32) * 0.02, 'W_q': jax.random.normal(ks[3], (HEADS * RET, H), jnp.float32) * 0.02, 'keys': jax.random.normal(ks[4], (HEADS, NUM_KEYS, 2, RET // 2), jnp.float32) * 0.02, 'down_embed': jax.random.normal(ks[5], (NUM_EXPERTS, H), jnp.float32) * 0.02, 'up_embed': jax.random.normal(ks[6], (NUM_EXPERTS, H), jnp.float32) * 0.02}
    _L0_ffn_in = _L0_ffn_setup()

    def _L1_attn_setup():
        import jax, jax.numpy as jnp
        import numpy as np
        B, S, H, D = (4, 512, 256, 256)
        key = jax.random.key(seed)
        k0, k1, k2, k3 = jax.random.split(key, 4)
        x = jax.random.normal(k0, (B, S, H), dtype=jnp.float32)
        scale = 1.0 / np.sqrt(H)
        Wq = jax.random.normal(k1, (D, H), dtype=jnp.float32) * scale
        Wk = jax.random.normal(k2, (D, H), dtype=jnp.float32) * scale
        Wv = jax.random.normal(k3, (D, H), dtype=jnp.float32) * scale
        return {'x': x, 'Wq': Wq, 'Wk': Wk, 'Wv': Wv}
    _L1_attn_in = _L1_attn_setup()

    def _L1_ffn_setup():
        import jax, jax.numpy as jnp
        import numpy as np
        DIM = 256

        def _reference_tuple_inner(x, W_r, W_k, W_v, mu_r, mu_k):
            B, T, C = x.shape
            x_prev = jnp.concatenate([jnp.zeros((B, 1, C), x.dtype), x[:, :-1, :]], axis=1)
            xr = mu_r * x + (1.0 - mu_r) * x_prev
            xk = mu_k * x + (1.0 - mu_k) * x_prev
            r = jax.nn.sigmoid(jnp.einsum('btc,dc->btd', xr, W_r))
            k = jnp.einsum('btc,dc->btd', xk, W_k)
            k_act = jnp.square(jax.nn.relu(k))
            out = r * jnp.einsum('btc,dc->btd', k_act, W_v)
            new_state = x[:, -1, :]
            return (out, new_state)
        key = jax.random.key(seed)
        ks = jax.random.split(key, 6)
        B, T, C = (8, 512, DIM)
        x = jax.random.normal(ks[0], (B, T, C), dtype=jnp.float32)
        s = 1.0 / np.sqrt(C)
        W_r = jax.random.uniform(ks[1], (C, C), jnp.float32, -s, s)
        W_k = jax.random.uniform(ks[2], (C, C), jnp.float32, -s, s)
        W_v = jax.random.uniform(ks[3], (C, C), jnp.float32, -s, s)
        mu_r = jax.random.uniform(ks[4], (C,), jnp.float32)
        mu_k = jax.random.uniform(ks[5], (C,), jnp.float32)
        return {'x': x, 'W_r': W_r, 'W_k': W_k, 'W_v': W_v, 'mu_r': mu_r, 'mu_k': mu_k}
    _L1_ffn_in = _L1_ffn_setup()
    _d = {'L0_attn_x': _L0_attn_in['x'], 'L0_attn_Wqkv': _L0_attn_in['Wqkv'], 'L0_attn_bqkv': _L0_attn_in['bqkv'], 'L0_attn_Wout': _L0_attn_in['Wout'], 'L0_attn_bout': _L0_attn_in['bout'], 'L0_ffn_W_up': _L0_ffn_in['W_up'], 'L0_ffn_W_down': _L0_ffn_in['W_down'], 'L0_ffn_W_q': _L0_ffn_in['W_q'], 'L0_ffn_keys': _L0_ffn_in['keys'], 'L0_ffn_down_embed': _L0_ffn_in['down_embed'], 'L0_ffn_up_embed': _L0_ffn_in['up_embed'], 'L1_attn_Wq': _L1_attn_in['Wq'], 'L1_attn_Wk': _L1_attn_in['Wk'], 'L1_attn_Wv': _L1_attn_in['Wv'], 'L1_ffn_W_r': _L1_ffn_in['W_r'], 'L1_ffn_W_k': _L1_ffn_in['W_k'], 'L1_ffn_W_v': _L1_ffn_in['W_v'], 'L1_ffn_mu_r': _L1_ffn_in['mu_r'], 'L1_ffn_mu_k': _L1_ffn_in['mu_k']}
    _x0 = _d['L0_attn_x']
    _d['L0_attn_x'] = jax.random.normal(jax.random.fold_in(jax.random.key(seed), 1), (16, 512, 256), dtype=_x0.dtype)
    del _x0
    return _d

def reference(L0_attn_x, L0_attn_Wqkv, L0_attn_bqkv, L0_attn_Wout, L0_attn_bout, L0_ffn_W_up, L0_ffn_W_down, L0_ffn_W_q, L0_ffn_keys, L0_ffn_down_embed, L0_ffn_up_embed, L1_attn_Wq, L1_attn_Wk, L1_attn_Wv, L1_ffn_W_r, L1_ffn_W_k, L1_ffn_W_v, L1_ffn_mu_r, L1_ffn_mu_k):

    def _L0_attn_ref(x, Wqkv, bqkv, Wout, bout):
        import jax, jax.numpy as jnp
        import numpy as np
        DIL = (1, 2, 4)
        SEG = (128, 128, 128)
        H = 16
        D = 256
        B, L = (2, 2048)

        def _mha(x, Wqkv, bqkv, Wo, bo):
            lead = x.shape[:-2]
            S = x.shape[-2]
            hd = D // H
            qkv = x @ Wqkv.T + bqkv
            q, k, v = jnp.split(qkv, 3, axis=-1)
            q = q.reshape(*lead, S, H, hd)
            k = k.reshape(*lead, S, H, hd)
            v = v.reshape(*lead, S, H, hd)
            scale = 1.0 / np.float32(np.sqrt(hd))
            scores = jnp.einsum('...qhd,...khd->...hqk', q, k) * scale
            a = jax.nn.softmax(scores, axis=-1)
            o = jnp.einsum('...hqk,...khd->...qhd', a, v).reshape(*lead, S, D)
            return o @ Wo.T + bo
        b_, L_, D_ = x.shape
        n = len(DIL)
        pairs = [(br, off) for br in range(n) for off in range(DIL[br])][:n]
        outs = []
        for br, off in pairs:
            r, S = (DIL[br], SEG[br])
            xs = x[:, off::r, :].reshape(b_, -1, S, D_)
            att = _mha(xs, Wqkv[br], bqkv[br], Wout[br], bout[br])
            full = jnp.zeros_like(x).at[:, off::r, :].set(att.reshape(b_, -1, D_))
            outs.append(full)
        w = jax.nn.softmax(jnp.full((n,), 1.0 / n, dtype=x.dtype))
        res = outs[0] * w[0]
        for i in range(1, n):
            res = res + w[i] * outs[i]
        return res

    def _L0_ffn_ref(hidden_states, W_up, W_down, W_q, keys, down_embed, up_embed):
        import jax, jax.numpy as jnp
        import numpy as np
        B, T, H = (2, 512, 256)
        I = 1024
        HEADS = 4
        RET = 128
        NUM_EXPERTS = 1024
        NUM_KEYS = 64
        K = 8
        b, t, hd = hidden_states.shape
        h, nk, _, n = keys.shape
        q = jnp.einsum('btd,ed->bte', hidden_states, W_q)
        q = q.reshape(b, t, 2, h, n).transpose(2, 0, 1, 3, 4)
        sim = jnp.einsum('pbthn,hkpn->pbthk', q, keys)
        scores_xy, idx_xy = jax.lax.top_k(sim, K)
        sx, sy = (scores_xy[0], scores_xy[1])
        ix, iy = (idx_xy[0], idx_xy[1])
        all_scores = (sx[..., :, None] + sy[..., None, :]).reshape(b, t, h, K * K)
        all_idx = (ix[..., :, None] * nk + iy[..., None, :]).reshape(b, t, h, K * K)
        scores, pk = jax.lax.top_k(all_scores, K)
        indices = jnp.take_along_axis(all_idx, pk, axis=-1)
        de = down_embed[indices]
        ue = up_embed[indices]
        w = jax.nn.silu(jnp.einsum('btd,bthkd->bthk', hidden_states, de) * jax.nn.softmax(scores, axis=-1))
        experts_states = jnp.einsum('bthk,bthkd->btd', w, ue)
        dense = jnp.einsum('bti,di->btd', jax.nn.silu(jnp.einsum('btd,id->bti', hidden_states, W_up)), W_down)
        return dense + experts_states

    def _L1_attn_ref(x, Wq, Wk, Wv):
        import jax, jax.numpy as jnp
        import numpy as np
        B, S, H, D = (4, 512, 256, 256)
        b, s, _ = x.shape
        d = Wq.shape[0]
        q = jnp.einsum('bsh,dh->bsd', x, Wq)
        k = jnp.einsum('bsh,dh->bsd', x, Wk)
        v = jnp.einsum('bsh,dh->bsd', x, Wv)
        kT = k.reshape(b, d, s)
        scores = jnp.matmul(q, kT) / jnp.sqrt(jnp.float32(d))
        attn = jax.nn.softmax(scores, axis=0)
        tril = jnp.tril(jnp.ones((s, s), dtype=bool))
        attn_masked = jnp.where(tril[None, :, :], attn, jnp.float32(1e-09))
        return jnp.matmul(attn_masked, v)

    def _L1_ffn_ref(x, W_r, W_k, W_v, mu_r, mu_k):
        import jax, jax.numpy as jnp
        import numpy as np
        DIM = 256

        def _reference_tuple_inner(x, W_r, W_k, W_v, mu_r, mu_k):
            B, T, C = x.shape
            x_prev = jnp.concatenate([jnp.zeros((B, 1, C), x.dtype), x[:, :-1, :]], axis=1)
            xr = mu_r * x + (1.0 - mu_r) * x_prev
            xk = mu_k * x + (1.0 - mu_k) * x_prev
            r = jax.nn.sigmoid(jnp.einsum('btc,dc->btd', xr, W_r))
            k = jnp.einsum('btc,dc->btd', xk, W_k)
            k_act = jnp.square(jax.nn.relu(k))
            out = r * jnp.einsum('btc,dc->btd', k_act, W_v)
            new_state = x[:, -1, :]
            return (out, new_state)
        return _reference_tuple_inner(x, W_r, W_k, W_v, mu_r, mu_k)[0]
    x = L0_attn_x
    x = x + 0.5 * _L0_ffn_ref(_layernorm(x, axis=-1), L0_ffn_W_up, L0_ffn_W_down, L0_ffn_W_q, L0_ffn_keys, L0_ffn_down_embed, L0_ffn_up_embed)
    x = x + _L0_attn_ref(_layernorm(x, axis=-1), L0_attn_Wqkv, L0_attn_bqkv, L0_attn_Wout, L0_attn_bout)
    x = x + 0.5 * _L0_ffn_ref(_layernorm(x, axis=-1), L0_ffn_W_up, L0_ffn_W_down, L0_ffn_W_q, L0_ffn_keys, L0_ffn_down_embed, L0_ffn_up_embed)
    x = x + 0.5 * _L1_ffn_ref(_layernorm(x, axis=-1), L1_ffn_W_r, L1_ffn_W_k, L1_ffn_W_v, L1_ffn_mu_r, L1_ffn_mu_k)
    x = x + _L1_attn_ref(_layernorm(x, axis=-1), L1_attn_Wq, L1_attn_Wk, L1_attn_Wv)
    x = x + 0.5 * _L1_ffn_ref(_layernorm(x, axis=-1), L1_ffn_W_r, L1_ffn_W_k, L1_ffn_W_v, L1_ffn_mu_r, L1_ffn_mu_k)
    return x

_drawn_inputs = setup_inputs


def setup_inputs(seed=0):
    import zlib

    import numpy as np

    out = dict(_drawn_inputs(seed))
    spreads = {'L0_attn_bqkv': (0.0, 0.1), 'L0_attn_bout': (0.0, 0.1)}
    factors = {'L0_ffn_W_q': 8.0,
     'L0_ffn_keys': 8.0,
     'L0_ffn_down_embed': 4.316,
     'L0_ffn_up_embed': 4.06,
     'L1_ffn_W_r': 4.24,
     'L1_ffn_mu_r': 8.0}
    for name, (base, spread) in spreads.items():
        noise = np.random.default_rng([zlib.crc32(name.encode()), seed]).standard_normal(out[name].shape)
        drawn = base * np.exp(spread * noise) if base else spread * noise
        out[name] = jnp.asarray(drawn.astype(out[name].dtype))
    for name, factor in factors.items():
        out[name] = (out[name] * factor).astype(out[name].dtype)
    return out
```

```python
from contextlib import ExitStack

import numpy as np
import concourse.bass as bass
from concourse import mybir
from concourse.alu_op_type import AluOpType as ALU

ACT = mybir.ActivationFunctionType
AX = mybir.AxisListType
F32 = mybir.dt.float32
F32R = mybir.dt.float32r

P = 128
B, S, D = 16, 512, 256
N = B * S
DC = D // P
EPS = 1e-5


class Turn:

    def __init__(self, group, step, unroll):
        self.group, self.step, self.unroll = group + step // unroll if step // unroll else group, step % unroll, unroll

    def __add__(self, k):
        return Turn(self.group, self.step + k, self.unroll)

    def __sub__(self, k):
        return self + (-k)

    def exists(self, first=0, last=None):
        if not isinstance(self.group, int):
            return True
        n = self.group * self.unroll + self.step
        return n >= first and (last is None or n < last)

    def times(self, per, plus):
        return self.group * (self.unroll * per) + (self.step * per + plus)

    def rows(self, size, offset=0, count=None):
        return bass.ds(self.times(size, offset), size if count is None else count)


class Track:

    def __init__(self, sem, *marks, inc=1):
        self.sem, self.marks, self.inc = sem, marks, inc

    def mark(self, instruction, name=None):
        assert name is None or name in self.marks
        instruction.then_inc(self.sem, self.inc)

    def wait(self, engine, turn, name=None, alone=False):
        at = self.marks.index(name) + 1 if name else len(self.marks)
        n = len(self.marks) * self.inc
        engine.wait_ge(self.sem, turn.times(n, at * self.inc))
        if alone:
            engine.nop(nofuse=True)


def turns(engine, count, unroll, step):
    groups = count // unroll
    assert groups * unroll == count and groups >= 2
    for u in range(unroll):
        step(Turn(0, u, unroll))
    if groups > 2:
        with engine.Fori(1, groups - 1) as g:
            for u in range(unroll):
                step(Turn(g, u, unroll))
    for u in range(unroll):
        step(Turn(groups - 1, u, unroll))


class Memory:

    def __init__(self, nc, ctx, name):
        self.nc, self.ctx, self.name = nc, ctx, name

    def sbuf(self, name, *shape, dt=F32):
        return self.ctx.enter_context(self.nc.sbuf_tensor(f"{self.name}_{name}", [P, *shape], dt))

    def psum(self, name, *shape):
        return self.ctx.enter_context(self.nc.psum_tensor(f"{self.name}_{name}", [P, *shape], F32))

    def sem(self, name):
        return self.ctx.enter_context(self.nc.semaphore(f"{self.name}_{name}"))

    def track(self, name, *marks, inc=1):
        return Track(self.sem(name), *(marks or (name,)), inc=inc)


def matmul_split(pe, out, lhs, rhs, start, stop):
    (lh, ll), (rh, rl) = lhs, rhs
    pe.matmul(out, lh, rl, start=start, stop=False)
    pe.matmul(out, ll, rh, start=False, stop=False)
    return pe.matmul(out, lh, rh, start=False, stop=stop)


def load_split(nc, m, loads, heads=None):
    stage = [m.sbuf(f"stage{k}", 1024) for k in range(2)]
    s_ld = [m.sem(f"s_stage{k}") for k in range(2)]
    s_z, s_hi, s_lo = m.sem("s_zero"), m.sem("s_hi"), m.sem("s_lo")
    with nc.Block() as block:
        @block.sync
        def _(sp):
            sp.wait_ge(s_z, 2)
            for n, (src, hi, lo) in enumerate(loads):
                if n >= 2:
                    sp.wait_ge(s_lo, n - 1)
                raw = stage[n % 2][:, 0:hi.shape[1]]
                if heads:
                    raw = raw.rearrange("p (h s) -> p h s", s=heads[1])[:, :, 0:heads[0]]
                    src = src.rearrange("p (h d) -> p h d", d=heads[0])
                sp.dma_start(raw, src).then_inc(s_ld[n % 2], 16)

        @block.vector
        def _(dve):
            for k in range(2):
                dve.memset(stage[k][:], 0.0).then_inc(s_z, 1)
            for n, (src, hi, lo) in enumerate(loads):
                raw = stage[n % 2][:, 0:hi.shape[1]]
                dve.wait_ge(s_ld[n % 2], 16 * (n // 2 + 1))
                dve.tensor_copy(hi, raw).then_inc(s_hi, 1)
                dve.wait_ge(s_hi, n + 1)
                dve.tensor_tensor(lo, raw, hi.bitcast(F32), ALU.subtract).then_inc(s_lo, 1)


class Norm:

    def __init__(self, m, tiles, x_of, half):
        self.tiles, self.x_of, self.half = tiles, x_of, half
        self.bs, self.mv = m.sbuf("bs", 2, tiles, 6), m.sbuf("mv", 2, tiles, 2)
        self.ve, self.rstd = m.sbuf("ve", 2, tiles), m.sbuf("rstd", 2, tiles)
        self.d_ln = m.track("d_ln", "bn", "mv")
        self.g_ln = m.track("g_ln", "ve", "rstd")
        self.d_h = m.track("d_h")

    def statistics(self, dve, t):
        k, x = t.step % 2, self.x_of(t)
        for v in range(self.tiles):
            last = dve.bn_stats(self.bs[:, k, v, :], x[:, v, :])
        self.d_ln.mark(last, "bn")
        self.d_ln.wait(dve, t, "bn", alone=True)
        for v in range(self.tiles):
            last = dve.bn_aggr(self.mv[:, k, v, :], self.bs[:, k, v, :])
        self.d_ln.mark(last, "mv")

    def root(self, pool, t):
        k = t.step % 2
        self.d_ln.wait(pool, t, "mv", alone=True)
        self.g_ln.mark(pool.tensor_scalar(self.ve[:, k, :], self.mv[:, k, :, 1], EPS, None, ALU.add), "ve")
        self.g_ln.wait(pool, t, "ve")
        self.g_ln.mark(pool.tensor_tensor(self.rstd[:, k, :], self.ve[:, k, :],
                                          self.half[:, 0:1].to_broadcast([P, self.tiles]), ALU.pow), "rstd")

    def scale(self, dve, t, h):
        k, x = t.step % 2, self.x_of(t)
        self.g_ln.wait(dve, t, "rstd")
        for v in range(self.tiles):
            last = dve.tensor_scalar(h[:, v, :], x[:, v, :], self.mv[:, k, v, 0:1],
                                     self.rstd[:, k, v:v + 1], ALU.subtract, ALU.mult)
        self.d_h.mark(last)


def slot_wait(e, tracks, t):
    k = len(tracks)
    e.wait_ge(tracks[t.step % k].sem, t.group * (16 * (t.unroll // k)) + 16 * (t.step // k + 1))


def row_tiles(a, t):
    return a[t.rows(S), :].rearrange("(v p) d -> p v d", p=P)


HEADS, KEYS, TOP = 4, 64, 8
EXPERTS, HID = 1024, 1024
XROWS = EXPERTS // KEYS
GRID = EXPERTS + TOP * TOP
V = 2
EC = EXPERTS // P


def expert_ffn(nc, name, src, dst, w):
    with ExitStack() as ctx:
        m = Memory(nc, ctx, name)
        ws = [m.sbuf(f"ws{k}", DC, 2 * HEADS * KEYS, dt=F32R) for k in "hl"]
        wdown = [m.sbuf(f"wdown{k}", DC, EXPERTS, dt=F32R) for k in "hl"]
        wup = [m.sbuf(f"wup{k}", DC, HID, dt=F32R) for k in "hl"]
        eup = m.sbuf("eup", EC, D)
        wdn = m.sbuf("wdn", HID // P, D)
        ident, half = m.sbuf("ident", P), m.sbuf("half", 1)
        with ExitStack() as sub:
            ms = Memory(nc, sub, name + "w")
            fold = ms.sbuf("fold", DC, 2 * HEADS * KEYS)
            s_q, s_z, s_f, s_fc = ms.sem("s_q"), ms.sem("s_z"), ms.sem("s_f"), ms.sem("s_fc")
            wq = ms.sbuf("wq", 4, D)
            kt = ms.sbuf("kt", 4, P)
            pf = ms.psum("pf", DC, 2 * HEADS * KEYS)
            with nc.Block() as block:
                @block.vector
                def _(dve):
                    dve.memset(kt[:], 0.0).then_inc(s_z, 1)
                    dve.memset(half[:], -0.5).then_inc(s_z, 1)
                    dve.wait_ge(s_f, 1)
                    dve.tensor_copy(fold[:], pf[:]).then_inc(s_fc, 1)
                    dve.wait_ge(s_fc, 1)
                    dve.tensor_copy(ws[0][:], fold[:]).then_inc(s_fc, 1)
                    dve.wait_ge(s_fc, 2)
                    dve.tensor_tensor(ws[1][:], fold[:], ws[0][:].bitcast(F32), ALU.subtract).then_inc(s_fc, 1)

                @block.sync
                def _(sp):
                    sp.dma_start(ident[:], w["ident"]).then_inc(s_q, 16)
                    sp.dma_start(wq[:], w["wq"].rearrange("(e p) c -> p e c", p=P)).then_inc(s_q, 16)
                    sp.dma_start(eup[:], w["up_embed"].rearrange("(e p) d -> p e d", p=P)).then_inc(s_q, 16)
                    sp.dma_start(wdn[:], w["wdn"].rearrange("(e p) d -> p e d", p=P)).then_inc(s_q, 16)
                    sp.wait_ge(s_z, 1)
                    for g in range(2 * HEADS):
                        r = (g % 2) * KEYS
                        sp.dma_start(kt[r:r + KEYS, g // 2, r:r + KEYS], w["keys"][g]).then_inc(s_q, 16)
                    sp.wait_ge(s_q, 16 * 12)

                @block.tensor
                def _(pe):
                    pe.wait_ge(s_q, 16 * 12)
                    for c in range(DC):
                        for e in range(4):
                            mm = pe.matmul(pf[:, c, e * P:(e + 1) * P], wq[:, e, c * P:(c + 1) * P],
                                           kt[:, e, :], start=True, stop=True)
                    mm.then_inc(s_f, 1)
            load_split(nc, ms, [(w[n][c * P:(c + 1) * P, :], t[0][:, c, :], t[1][:, c, :])
                                for n, t in (("wdown", wdown), ("wup", wup)) for c in range(DC)])

        xt = [m.sbuf(f"xt{k}", V, D) for k in range(4)]
        yt = [m.sbuf(f"yt{k}", V, D) for k in range(2)]
        h = m.sbuf("h", V, D)
        hT = [[m.sbuf(f"hT{r}{k}", DC, V * P, dt=F32R) for k in "hl"] for r in range(2)]
        sim = m.sbuf("sim", V, 2 * HEADS * KEYS)
        tx, ty, tc, tp, tm, te = (m.sbuf(k, V, HEADS, TOP) for k in ("tx", "ty", "tc", "tp", "tm", "te"))
        cand = m.sbuf("cand", V, HEADS, TOP * TOP)
        negm, z, rz = (m.sbuf(k, V, HEADS) for k in ("negm", "z", "rz"))
        p_last = m.sbuf("p_last", V)
        grid = [m.sbuf(f"grid{v}", HEADS, GRID) for v in range(V)]
        q = [m.sbuf(f"q{v}", HEADS, GRID) for v in range(V)]
        clamped = m.sbuf("clamped", V)
        wT = [m.sbuf(f"wT{v}", EC, P) for v in range(V)]
        hs = m.sbuf("hs", HID // P, V * P)

        p_tr, p_sim, p_out, p_h = (m.psum(k, 512) for k in ("p_tr", "p_sim", "p_out", "p_h"))
        p_hid = (p_h, p_tr)
        p_dot, p_wT = m.psum("p_dot", EXPERTS), m.psum("p_wT", EC, P)

        s_ld = [m.track(f"s_ld{k}", inc=16) for k in range(4)]
        s_st = [m.track(f"s_st{k}", inc=16) for k in range(2)]
        norm = Norm(m, V, lambda t: xt[t.step % 4], half)
        t_hT = m.track("t_hT")
        a_hT, d_hT = m.track("a_hT"), m.track("d_hT")
        t_sim = m.track("t_sim", "0", "1")
        a_sim = m.track("a_sim", "0", "1")
        d_top = m.track("d_top", "maxes", "cand", "clamped pairs", "best", "negm", "tm")
        a_te = m.track("a_te")
        d_z = m.track("d_z", "z", "rz")
        g_grid = m.track("g_grid", "0", "1")
        t_dot = m.track("t_dot", "0", "1")
        d_last = m.track("d_last", "0", "1")
        d_mask = m.track("d_mask", "0", "1")
        a_exp = m.track("a_exp", "0", "1")
        d_mul = m.track("d_mul", "0", "1")
        a_silu = m.track("a_silu", "0", "1")
        d_clamp = m.track("d_clamp", "sum0", "add0", "sum1", "add1")
        t_hid = m.track("t_hid", *(str(k) for k in range(4)))
        a_hid = m.track("a_hid", *(str(k) for k in range(4)))
        t_wT = m.track("t_wT", "0", "1")
        a_wT = m.track("a_wT", "0", "1")
        t_out = m.track("t_out", "0", "1")
        d_out = m.track("d_out", "0", "1")

        count, unroll = N // (V * P), 4
        rows = lambda a, t: a[t.rows(V * P), :].rearrange("(v p) d -> p v d", p=P)

        with nc.Block() as block:
            @block.sync
            def _(sp):
                def load(t):
                    k = t.step % 4
                    sp.dma_start(xt[k][:], rows(src, t)).then_inc(s_ld[k].sem, 16)

                def store(t):
                    k = t.step % 2
                    d_out.wait(sp, t, "1")
                    sp.dma_start(rows(dst, t), yt[k][:]).then_inc(s_st[k].sem, 16)

                for n in range(3):
                    load(Turn(0, n, unroll))

                def step(t):
                    if (t - 1).exists():
                        store(t - 1)
                    if (t + 3).exists(last=count):
                        load(t + 3)
                turns(sp, count, unroll, step)
                store(Turn(0, count - 1, unroll))
                for k in range(2):
                    sp.wait_ge(s_st[k].sem, 16 * (count // 2))

            @block.gpsimd
            def _(pool):
                def scores(t, v):
                    a_sim.wait(pool, t, str(v))
                    if (t - 1).exists():
                        d_mul.wait(pool, t - 1, str(v))
                    sx = sim[:, v, 0:HEADS * KEYS].rearrange("p (h k) -> p h k", h=HEADS)[:, :, 0:XROWS]
                    sy = sim[:, v, HEADS * KEYS:].rearrange("p (h k) -> p h k", h=HEADS)
                    for hd in range(HEADS):
                        last = pool.tensor_tensor(
                            grid[v][:, hd, 0:EXPERTS].rearrange("p (i j) -> p i j", i=XROWS),
                            sx[:, hd, :].unsqueeze(2).to_broadcast([P, XROWS, KEYS]),
                            sy[:, hd, :].unsqueeze(1).to_broadcast([P, XROWS, KEYS]), ALU.add)
                    g_grid.mark(last, str(v))

                norm.root(pool, Turn(0, 0, unroll))
                norm.root(pool, Turn(0, 1, unroll))

                def step(t):
                    scores(t, 0)
                    scores(t, 1)
                    if (t + 2).exists(last=count):
                        norm.root(pool, t + 2)
                turns(pool, count, unroll, step)

            @block.tensor
            def _(pe):
                def turn_h(t):
                    norm.d_h.wait(pe, t)
                    if (t - 1).exists():
                        d_hT.wait(pe, t - 1)
                    if (t - 2).exists():
                        a_hid.wait(pe, t - 2, "3")
                    for v in range(V):
                        for c in range(DC):
                            last = pe.transpose(p_tr[:, (c * V + v) * P:(c * V + v + 1) * P],
                                                h[:, v, c * P:(c + 1) * P], ident[:])
                    t_hT.mark(last)

                def similar(t):
                    a_hT.wait(pe, t)
                    d_hT.wait(pe, t)
                    for v in range(V):
                        if v:
                            a_sim.wait(pe, t, "0")
                        elif (t - 1).exists():
                            a_sim.wait(pe, t - 1, "1")
                        for c in range(DC):
                            last = matmul_split(pe, p_sim[:], [x[:, c, v * P:(v + 1) * P] for x in hT[t.step % 2]],
                                                [x[:, c, :] for x in ws], c == 0, c == DC - 1)
                        t_sim.mark(last, str(v))

                def dots(t, v):
                    if v:
                        d_mask.wait(pe, t, "0")
                    elif (t - 1).exists():
                        d_mask.wait(pe, t - 1, "1")
                    for e in range(2):
                        for c in range(DC):
                            last = matmul_split(pe, p_dot[:, e * 512:(e + 1) * 512],
                                                [x[:, c, v * P:(v + 1) * P] for x in hT[t.step % 2]],
                                                [x[:, c, e * 512:(e + 1) * 512] for x in wdown],
                                                c == 0, c == DC - 1)
                    t_dot.mark(last, str(v))

                def hidden(t, k):
                    if k >= 2:
                        a_hid.wait(pe, t, str(k - 2))
                    elif (t - 1).exists():
                        a_hid.wait(pe, t - 1, str(k + 2))
                    if k == 1:
                        d_hT.wait(pe, t + 1 if (t + 1).exists(last=count) else t)
                    for j in range(2):
                        i = 2 * k + j
                        for c in range(DC):
                            last = matmul_split(pe, p_hid[k % 2][:, j * V * P:(j + 1) * V * P],
                                                [x[:, c, i * P:(i + 1) * P] for x in wup],
                                                [x[:, c, :] for x in hT[t.step % 2]], c == 0, c == DC - 1)
                    t_hid.mark(last, str(k))

                def turn_w(t, v):
                    a_silu.wait(pe, t, str(v))
                    d_clamp.wait(pe, t, f"add{v}")
                    if v:
                        a_wT.wait(pe, t, "0")
                    elif (t - 1).exists():
                        a_wT.wait(pe, t - 1, "1")
                    for e in range(EC):
                        for hd in range(HEADS):
                            last = pe.matmul(p_wT[:, e, :], q[v][:, hd, e * P:(e + 1) * P], ident[:],
                                             is_transpose=True, start=hd == 0, stop=hd == HEADS - 1)
                    t_wT.mark(last, str(v))

                def output(t, v):
                    if v == 0:
                        a_hid.wait(pe, t, "3")
                    a_wT.wait(pe, t, str(v))
                    if v:
                        d_out.wait(pe, t, "0")
                    elif (t - 1).exists():
                        d_out.wait(pe, t - 1, "1")
                    o = p_out[:, v * D:(v + 1) * D]
                    for e in range(EC):
                        pe.matmul(o, hs[:, e, v * P:(v + 1) * P], wdn[:, e, :], start=e == 0, stop=False)
                    for e in range(EC):
                        last = pe.matmul(o, wT[v][:, e, :], eup[:, e, :], start=False, stop=e == EC - 1)
                    t_out.mark(last, str(v))

                first = Turn(0, 0, unroll)
                turn_h(first)
                similar(first)
                dots(first, 0)

                def step(t):
                    before, after = (t - 1).exists(), (t + 1).exists(last=count)
                    if before:
                        output(t - 1, 0)
                    dots(t, 1)
                    if after:
                        turn_h(t + 1)
                    if before:
                        output(t - 1, 1)
                    if after:
                        similar(t + 1)
                    for k in range(4):
                        hidden(t, k)
                    turn_w(t, 0)
                    if after:
                        dots(t + 1, 0)
                    turn_w(t, 1)
                turns(pe, count, unroll, step)
                end = Turn(0, count - 1, unroll)
                for v in range(V):
                    output(end, v)

            @block.scalar
            def _(act):
                def turn_h(t):
                    t_hT.wait(act, t)
                    if (t - 2).exists():
                        t_hid.wait(act, t - 2, "3")
                    a_hT.mark(act.copy(hT[t.step % 2][0][:].rearrange("p c n -> p (c n)"), p_tr[:]))

                def similar(t):
                    for v in range(V):
                        t_sim.wait(act, t, str(v))
                        if (t - 1).exists():
                            g_grid.wait(act, t - 1, str(v))
                            d_top.wait(act, t - 1, "tm")
                        a_sim.mark(act.copy(sim[:, v, :], p_sim[:]), str(v))

                def exps(t, v):
                    d_mask.wait(act, t, str(v))
                    if v == 0:
                        d_top.wait(act, t, "tm")
                        if (t - 1).exists():
                            d_z.wait(act, t - 1, "z")
                        a_te.mark(act.activation(te[:], tm[:], ACT.Exp))
                    for hd in range(HEADS):
                        last = act.activation(grid[v][:, hd, :], grid[v][:, hd, :], ACT.Exp,
                                              bias=negm[:, v, hd:hd + 1])
                    a_exp.mark(last, str(v))

                def turned(t, v):
                    t_wT.wait(act, t, str(v))
                    if (t - 1).exists():
                        t_out.wait(act, t - 1, str(v))
                    a_wT.mark(act.copy(wT[v][:], p_wT[:]), str(v))

                def hidden(t, k):
                    t_hid.wait(act, t, str(k))
                    if k == 0 and (t - 1).exists():
                        t_out.wait(act, t - 1, "1")
                    a_hid.mark(act.activation(hs[:, 2 * k:2 * k + 2, :],
                                              p_hid[k % 2][:].rearrange("p (j n) -> p j n", j=2), ACT.Silu), str(k))

                def weights(t, v):
                    d_mul.wait(act, t, str(v))
                    a_silu.mark(act.activation(q[v][:], q[v][:], ACT.Silu), str(v))

                first = Turn(0, 0, unroll)
                turn_h(first)
                similar(first)

                def step(t):
                    after = (t + 1).exists(last=count)
                    exps(t, 0)
                    if after:
                        turn_h(t + 1)
                    exps(t, 1)
                    if after:
                        similar(t + 1)
                    hidden(t, 0)
                    hidden(t, 1)
                    weights(t, 0)
                    hidden(t, 2)
                    hidden(t, 3)
                    weights(t, 1)
                    turned(t, 0)
                    turned(t, 1)
                turns(act, count, unroll, step)

            @block.vector
            def _(dve):
                def front(t):
                    slot_wait(dve, s_ld, t)
                    norm.statistics(dve, t)

                def normed(t):
                    if (t - 1).exists():
                        t_hT.wait(dve, t - 1)
                    norm.scale(dve, t, h)

                def turned(t):
                    a_hT.wait(dve, t)
                    x = hT[t.step % 2]
                    d_hT.mark(dve.tensor_tensor(x[1][:].rearrange("p c n -> p (c n)"), p_tr[:],
                                                x[0][:].rearrange("p c n -> p (c n)").bitcast(F32),
                                                ALU.subtract))

                def rank(t):
                    for v in range(V):
                        a_sim.wait(dve, t, str(v), alone=True)
                        for hd in range(HEADS):
                            sx = sim[:, v, hd * KEYS:(hd + 1) * KEYS]
                            sy = sim[:, v, (HEADS + hd) * KEYS:(HEADS + hd + 1) * KEYS]
                            dve.max(tx[:, v, hd, :], sx)
                            dve.max(ty[:, v, hd, :], sy)
                            last = dve.max(tc[:, v, hd, :], sx[:, XROWS:])
                    d_top.mark(last, "maxes")
                    d_top.wait(dve, t, "maxes")
                    if (t - 1).exists():
                        a_exp.wait(dve, t - 1, "1")
                    for v in range(V):
                        pairs = lambda a: a[:, v].unsqueeze(3).to_broadcast([P, HEADS, TOP, TOP])
                        across = ty[:, v].unsqueeze(2).to_broadcast([P, HEADS, TOP, TOP])
                        last = dve.tensor_tensor(cand[:, v].rearrange("p h (a b) -> p h a b", a=TOP),
                                                 pairs(tx), across, ALU.add)
                    d_top.mark(last, "cand")
                    for v in range(V):
                        if (t - 1).exists():
                            d_mul.wait(dve, t - 1, str(v))
                        last = dve.tensor_tensor(
                            grid[v][:, :, EXPERTS:].rearrange("p h (a b) -> p h a b", a=TOP),
                            tc[:, v].unsqueeze(3).to_broadcast([P, HEADS, TOP, TOP]),
                            ty[:, v].unsqueeze(2).to_broadcast([P, HEADS, TOP, TOP]), ALU.add)
                    d_top.mark(last, "clamped pairs")
                    d_top.wait(dve, t, "cand", alone=True)
                    for v in range(V):
                        for hd in range(HEADS):
                            last = dve.max(tp[:, v, hd, :], cand[:, v, hd, :])
                    d_top.mark(last, "best")
                    d_top.wait(dve, t, "best")
                    d_top.mark(dve.tensor_scalar(negm[:], tp[:, :, :, 0], -1.0, None, ALU.mult), "negm")
                    d_top.mark(dve.tensor_tensor(tm[:], tp[:], tp[:, :, :, 0:1].to_broadcast([P, V, HEADS, TOP]),
                                                 ALU.subtract), "tm")

                def mask(t, v):
                    t_dot.wait(dve, t, str(v))
                    g_grid.wait(dve, t, str(v))
                    if v == 0:
                        d_top.wait(dve, t, "tm")
                    if (t - 1).exists():
                        t_wT.wait(dve, t - 1, str(v))
                        d_clamp.wait(dve, t - 1, f"add{v}")
                    d_last.mark(dve.tensor_copy(p_last[:, v:v + 1], p_dot[:, EXPERTS - 1:EXPERTS]), str(v))
                    for hd in range(HEADS):
                        dve.scalar_tensor_tensor(out=q[v][:, hd, 0:EXPERTS], in0=grid[v][:, hd, 0:EXPERTS],
                                                 scalar=tp[:, v, hd, TOP - 1:TOP], in1=p_dot[:],
                                                 op0=ALU.is_ge, op1=ALU.mult)
                    d_last.wait(dve, t, str(v))
                    for hd in range(HEADS):
                        last = dve.tensor_scalar(q[v][:, hd, EXPERTS:], grid[v][:, hd, EXPERTS:],
                                                 tp[:, v, hd, TOP - 1:TOP], p_last[:, v:v + 1],
                                                 ALU.is_ge, ALU.mult)
                    d_mask.mark(last, str(v))

                def sums(t):
                    a_te.wait(dve, t)
                    d_z.mark(dve.tensor_reduce(z[:], te[:], AX.X, ALU.add), "z")
                    d_z.wait(dve, t, "z")
                    d_z.mark(dve.reciprocal(rz[:], z[:]), "rz")
                    d_z.wait(dve, t, "rz")

                def weigh(t, v):
                    d_mask.wait(dve, t, str(v))
                    a_exp.wait(dve, t, str(v))
                    for hd in range(HEADS):
                        last = dve.scalar_tensor_tensor(out=q[v][:, hd, :], in0=q[v][:, hd, :],
                                                        scalar=rz[:, v, hd:hd + 1], in1=grid[v][:, hd, :],
                                                        op0=ALU.mult, op1=ALU.mult)
                    d_mul.mark(last, str(v))

                def clamp(t, v):
                    a_silu.wait(dve, t, str(v))
                    d_clamp.mark(dve.tensor_reduce(clamped[:, v:v + 1], q[v][:, :, EXPERTS:], AX.XY, ALU.add), f"sum{v}")
                    d_clamp.wait(dve, t, f"sum{v}")
                    d_clamp.mark(dve.tensor_tensor(q[v][:, 0, EXPERTS - 1:EXPERTS], q[v][:, 0, EXPERTS - 1:EXPERTS],
                                                   clamped[:, v:v + 1], ALU.add), f"add{v}")

                def output(t, v):
                    t_out.wait(dve, t, str(v))
                    if v == 0 and (t - 2).exists():
                        slot_wait(dve, s_st, t - 2)
                    d_out.mark(dve.scalar_tensor_tensor(
                        out=yt[t.step % 2][:, v, :], in0=p_out[:, v * D:(v + 1) * D], scalar=0.5,
                        in1=xt[t.step % 4][:, v, :], op0=ALU.mult, op1=ALU.add), str(v))

                first = Turn(0, 0, unroll)
                front(first)
                normed(first)
                turned(first)
                front(first + 1)
                rank(first)
                normed(first + 1)

                def step(t):
                    before, after = (t - 1).exists(), (t + 1).exists(last=count)
                    mask(t, 0)
                    if before:
                        output(t - 1, 0)
                    if (t + 2).exists(last=count):
                        front(t + 2)
                    mask(t, 1)
                    if after:
                        turned(t + 1)
                    sums(t)
                    weigh(t, 0)
                    weigh(t, 1)
                    if before:
                        output(t - 1, 1)
                    if (t + 2).exists(last=count):
                        normed(t + 2)
                    clamp(t, 0)
                    if after:
                        rank(t + 1)
                    clamp(t, 1)
                turns(dve, count, unroll, step)
                end = Turn(0, count - 1, unroll)
                output(end, 0)
                output(end, 1)


def channel_mix(nc, name, src, dst, w):
    with ExitStack() as ctx:
        m = Memory(nc, ctx, name)
        T = S // P
        wr, wk, wv = (m.sbuf(k, DC, D) for k in ("wr", "wk", "wv"))
        mu = m.sbuf("mu", 2, DC)
        ident, half = m.sbuf("ident", P), m.sbuf("half", 1)
        xt = [m.sbuf(f"xt{k}", T, D) for k in range(4)]
        yt = [m.sbuf(f"yt{k}", T, D) for k in range(2)]
        h = m.sbuf("h", T, D)
        hT = m.sbuf("hT", DC, 1 + S)
        diff = m.sbuf("diff", DC, S)
        xr, xk = m.sbuf("xr", DC, S), m.sbuf("xk", DC, S)
        rs, ks, rk = m.sbuf("rs", T, D), m.sbuf("ks", DC, S), m.sbuf("rk", T, D)
        p_tr, p_k = m.psum("p_tr", DC, S), m.psum("p_k", DC, S)
        p_r, p_v = m.psum("p_r", T, D), m.psum("p_v", T, D)

        s_w, s_z = m.sem("s_w"), m.sem("s_z")
        s_ld = [m.track(f"s_ld{k}", inc=16) for k in range(4)]
        s_st = [m.track(f"s_st{k}", inc=16) for k in range(2)]
        norm = Norm(m, T, lambda t: xt[t.step % 4], half)
        t_hT, a_hT = m.track("t_hT"), m.track("a_hT")
        d_mix = m.track("d_mix", "diff", "xk", "xr")
        t_k, t_r, t_v = m.track("t_k"), m.track("t_r"), m.track("t_v")
        a_k = m.track("a_k", "relu", "square")
        a_r = m.track("a_r")
        d_out = m.track("d_out", "rk", "y")
        count, unroll = B, 4

        with nc.Block() as block:
            @block.sync
            def _(sp):
                for n, (t, k) in enumerate(((wr, "wr"), (wk, "wk"), (wv, "wv"))):
                    sp.dma_start(t[:], w[k].rearrange("(c p) d -> p c d", p=P)).then_inc(s_w, 16)
                sp.dma_start(ident[:], w["ident"]).then_inc(s_w, 16)
                with nc.allow_non_contiguous_dma(reason="256 words, once"):
                    for n, k in enumerate(("mu_r", "mu_k")):
                        sp.dma_start(mu[:, n, :], w[k].rearrange("(c p) -> p c", p=P)).then_inc(s_w, 16)

                def load(t):
                    sp.dma_start(xt[t.step % 4][:], row_tiles(src, t)).then_inc(s_ld[t.step % 4].sem, 16)

                def store(t):
                    d_out.wait(sp, t, "y")
                    sp.dma_start(row_tiles(dst, t), yt[t.step % 2][:]).then_inc(s_st[t.step % 2].sem, 16)

                for n in range(3):
                    load(Turn(0, n, unroll))

                def step(t):
                    if (t - 1).exists():
                        store(t - 1)
                    if (t + 3).exists(last=count):
                        load(t + 3)
                turns(sp, count, unroll, step)
                store(Turn(0, count - 1, unroll))
                for k in range(2):
                    sp.wait_ge(s_st[k].sem, 16 * (count // 2))

            @block.gpsimd
            def _(pool):
                pool.wait_ge(s_z, 2)
                norm.root(pool, Turn(0, 0, unroll))

                def step(t):
                    if (t + 1).exists(last=count):
                        norm.root(pool, t + 1)
                turns(pool, count, unroll, step)

            @block.tensor
            def _(pe):
                pe.wait_ge(s_w, 16 * 6)

                def turn_h(t):
                    norm.d_h.wait(pe, t)
                    if (t - 1).exists():
                        a_hT.wait(pe, t - 1)
                    for v in range(T):
                        for c in range(DC):
                            last = pe.transpose(p_tr[:, c, v * P:(v + 1) * P], h[:, v, c * P:(c + 1) * P], ident[:])
                    t_hT.mark(last)

                def keys(t):
                    d_mix.wait(pe, t, "xk")
                    if (t - 1).exists():
                        a_k.wait(pe, t - 1, "relu")
                    for i in range(DC):
                        for c in range(DC):
                            last = pe.matmul(p_k[:, i, :], wk[:, c, i * P:(i + 1) * P], xk[:, c, :],
                                             start=c == 0, stop=c == DC - 1)
                    t_k.mark(last)

                def receptance(t):
                    d_mix.wait(pe, t, "xr")
                    if (t - 1).exists():
                        a_r.wait(pe, t - 1)
                    for v in range(T):
                        for c in range(DC):
                            last = pe.matmul(p_r[:, v, :], xr[:, c, v * P:(v + 1) * P], wr[:, c, :],
                                             start=c == 0, stop=c == DC - 1)
                    t_r.mark(last)

                def values(t):
                    a_k.wait(pe, t, "square")
                    if (t - 1).exists():
                        d_out.wait(pe, t - 1, "rk")
                    for v in range(T):
                        for c in range(DC):
                            last = pe.matmul(p_v[:, v, :], ks[:, c, v * P:(v + 1) * P], wv[:, c, :],
                                             start=c == 0, stop=c == DC - 1)
                    t_v.mark(last)

                turn_h(Turn(0, 0, unroll))

                def step(t):
                    keys(t)
                    receptance(t)
                    if (t + 1).exists(last=count):
                        turn_h(t + 1)
                    values(t)
                turns(pe, count, unroll, step)

            @block.scalar
            def _(act):
                act.wait_ge(s_z, 1)

                def turned(t):
                    t_hT.wait(act, t)
                    if (t - 1).exists():
                        d_mix.wait(act, t - 1, "xr")
                    a_hT.mark(act.copy(hT[:, :, 1:], p_tr[:]))

                turned(Turn(0, 0, unroll))

                def step(t):
                    t_k.wait(act, t)
                    if (t - 1).exists():
                        t_v.wait(act, t - 1)
                    a_k.mark(act.activation(ks[:], p_k[:], ACT.Relu), "relu")
                    a_k.wait(act, t, "relu")
                    a_k.mark(act.activation(ks[:], ks[:], ACT.Square), "square")
                    t_r.wait(act, t)
                    if (t - 1).exists():
                        d_out.wait(act, t - 1, "rk")
                    a_r.mark(act.activation(rs[:], p_r[:], ACT.Sigmoid))
                    if (t + 1).exists(last=count):
                        turned(t + 1)
                turns(act, count, unroll, step)

            @block.vector
            def _(dve):
                dve.memset(hT[:, :, 0:1], 0.0).then_inc(s_z, 1)
                dve.memset(half[:], -0.5).then_inc(s_z, 1)
                dve.wait_ge(s_w, 16 * 6)

                def mix(t):
                    a_hT.wait(dve, t)
                    d_mix.mark(dve.tensor_tensor(diff[:], hT[:, :, 1:], hT[:, :, 0:S], ALU.subtract), "diff")
                    d_mix.wait(dve, t, "diff")
                    for n, out, free, mark in ((1, xk, t_k, "xk"), (0, xr, t_r, "xr")):
                        if (t - 1).exists():
                            free.wait(dve, t - 1)
                        for c in range(DC):
                            last = dve.scalar_tensor_tensor(out=out[:, c, :], in0=diff[:, c, :], scalar=mu[:, n, c:c + 1],
                                                            in1=hT[:, c, 0:S], op0=ALU.mult, op1=ALU.add)
                        d_mix.mark(last, mark)

                def output(t):
                    t_v.wait(dve, t)
                    a_r.wait(dve, t)
                    if (t - 1).exists():
                        d_out.wait(dve, t - 1, "y")
                    d_out.mark(dve.tensor_tensor(rk[:], p_v[:], rs[:], ALU.mult), "rk")
                    d_out.wait(dve, t, "rk")
                    if (t - 2).exists():
                        slot_wait(dve, s_st, t - 2)
                    d_out.mark(dve.scalar_tensor_tensor(
                        out=yt[t.step % 2][:], in0=rk[:], scalar=0.5, in1=xt[t.step % 4][:],
                        op0=ALU.mult, op1=ALU.add), "y")

                def front(t):
                    slot_wait(dve, s_ld, t)
                    norm.statistics(dve, t)
                    if (t - 1).exists():
                        t_hT.wait(dve, t - 1)
                    norm.scale(dve, t, h)

                front(Turn(0, 0, unroll))
                mix(Turn(0, 0, unroll))

                def step(t):
                    if (t + 1).exists(last=count):
                        front(t + 1)
                        mix(t + 1)
                    output(t)
                turns(dve, count, unroll, step)


MH, HD = 16, D // 16
SLOT = 32
BR = 2
SEGS = S // P
QB = 4
BRANCH_WEIGHT = float(np.float32(1) / np.float32(3))


def dilated_attention(nc, name, src, dst, w):
    with ExitStack() as ctx:
        m = Memory(nc, ctx, name)
        UR = BR * SEGS
        PADW = MH * SLOT
        wq, wk = ([[m.sbuf(f"w{n}{br}{k}", DC, PADW, dt=F32R) for k in "hl"] for br in range(BR)] for n in "qk")
        wv = [[m.sbuf(f"wv{br}{k}", DC, D, dt=F32R) for k in "hl"] for br in range(BR)]
        wo = m.sbuf("wo", BR, 4, D)
        sel = m.sbuf("sel", P)
        bq, bk = m.sbuf("bq", BR, 4), m.sbuf("bk", BR, 4)
        bqs, bk1 = m.sbuf("bqs", BR, 4), m.sbuf("bk1", BR, 4)
        kone = m.sbuf("kone", 1)
        bv, bo, bos = m.sbuf("bv", BR, D), m.sbuf("bo", BR, D), m.sbuf("bos", 2, D)
        ident, half = m.sbuf("ident", P), m.sbuf("half", 1)
        with ExitStack() as sub:
            load_split(nc, Memory(nc, sub, name + "a"),
                       [(w[n][br, c * P:(c + 1) * P, :], t[br][0][:, c, :], t[br][1][:, c, :])
                        for n, t in (("aq", wq), ("ak", wk)) for br in range(BR) for c in range(DC)], heads=(HD, SLOT))
        with ExitStack() as sub:
            load_split(nc, Memory(nc, sub, name + "b"),
                       [(w["av"][br, c * P:(c + 1) * P, :], wv[br][0][:, c, :], wv[br][1][:, c, :])
                        for br in range(BR) for c in range(DC)])

        xt = [m.sbuf(f"xt{k}", SEGS, D) for k in range(2)]
        xb = [m.sbuf(f"xb{k}", SEGS, D) for k in range(2)]
        yt = [m.sbuf(f"yt{k}", SEGS, D) for k in range(2)]
        h = m.sbuf("h", SEGS, D)
        hT = [[m.sbuf(f"hT{r}{k}", DC, S, dt=F32R) for k in "hl"] for r in range(2)]
        qT = [m.sbuf(f"qT{br}", 4, S) for br in range(BR)]
        kT = [m.sbuf(f"kT{br}", 4, S) for br in range(BR)]
        va = [m.sbuf(f"va{br}", SEGS, MH, SLOT) for br in range(BR)]
        mpad = m.sbuf("mpad", 4, P)
        qa = m.sbuf("qa", 4, P)
        ex = m.sbuf("ex", 4, 4, P)
        av = m.sbuf("av", 4, P)
        den, rden = m.sbuf("den", 4, P), m.sbuf("rden", 4, P)
        oT = [[m.sbuf(f"oT{r}{br}", 4, S) for br in range(BR)] for r in range(2)]

        p_s = [m.psum(f"p_s{b}", 4, P) for b in range(4)]
        p_m, p_av, p_pr, p_x = (m.psum(k, 512) for k in ("p_m", "p_av", "p_pr", "p_x"))

        s_w, s_z, s_c = m.sem("s_w"), m.sem("s_z"), m.sem("s_c")
        rows, units = B, B * UR
        WEIGHT_DMAS = 3 + BR * (2 + 4 * 3)
        s_ld = [m.track(f"s_ld{k}", inc=16) for k in range(2)]
        s_st = [m.track(f"s_st{k}", inc=16) for k in range(2)]
        norm = Norm(m, SEGS, lambda r: xt[r.step % 2], half)
        g_xb = m.track("g_xb")
        t_hT, a_hT, d_hT = (m.track(k, "0", "1") for k in ("t_hT", "a_hT", "d_hT"))
        t_q, t_k, t_v, a_q, a_k, d_v = (m.track(k) for k in ("t_q", "t_k", "t_v", "a_q", "a_k", "d_v"))
        banks = [str(b) for b in range(4)]
        t_s, d_max, t_st, a_ex = (m.track(k, *banks) for k in ("t_s", "d_max", "t_st", "a_ex"))
        t_m, d_qa, t_av = m.track("t_m"), m.track("d_qa"), m.track("t_av")
        a_av, t_den, a_den = (m.track(k) for k in ("a_av", "t_den", "a_den"))
        d_rden, g_o = m.track("d_rden"), m.track("g_o")
        t_y, d_y = m.track("t_y", *banks), m.track("d_y", *banks)

        row_of = lambda t: Turn(t.group, t.step // UR, 2)
        ur_of = lambda t: t.step % UR
        first_unit, first_row = Turn(0, 0, 2 * UR), Turn(0, 0, 2)
        OUT_AT = 2

        def tokens(a, br, n, count):
            if br == 0:
                return a[:, n:n + count]
            return a.rearrange("p (k two) -> p two k", two=2)[:, n // (S // 2):(n + count - 1) // (S // 2) + 1,
                                                              n % (S // 2):(n % (S // 2)) + min(count, S // 2)]

        with nc.Block() as block:
            @block.sync
            def _(sp):
                sp.dma_start(ident[:], w["ident"]).then_inc(s_w, 16)
                sp.dma_start(kone[:], w["kone"]).then_inc(s_w, 16)
                sp.dma_start(sel[:], w["sel"]).then_inc(s_w, 16)
                for br in range(BR):
                    sp.dma_start(bv[:, br, :], w["abv"][br:br + 1, :].to_broadcast([P, D])).then_inc(s_w, 16)
                    sp.dma_start(bo[:, br, :], w["abo"][br:br + 1, :].to_broadcast([P, D])).then_inc(s_w, 16)
                sp.wait_ge(s_z, 3)
                for br in range(BR):
                    for b in range(4):
                        for t, k in ((bq, "abq"), (bk, "abk")):
                            sp.dma_start(t[SLOT * b:SLOT * b + HD, br, :], w[k][br, b]).then_inc(s_w, 16)
                        sp.dma_start(wo[SLOT * b:SLOT * b + HD, br, :, :],
                                     w["ao"][br].rearrange("(c b d) e -> b d c e", b=4, d=HD)[b]).then_inc(s_w, 16)

                def load(r):
                    sp.dma_start(xt[r.step % 2][:], row_tiles(src, r)).then_inc(s_ld[r.step % 2].sem, 16)

                load(first_row)
                load(first_row + 1)

                def store(r):
                    d_y.wait(sp, r)
                    sp.dma_start(row_tiles(dst, r), yt[r.step % 2][:]).then_inc(s_st[r.step % 2].sem, 16)

                def step(r):
                    if (r + 2).exists(last=rows):
                        norm.d_h.wait(sp, r)
                        g_xb.wait(sp, r)
                        load(r + 2)
                    if (r - 1).exists():
                        store(r - 1)
                turns(sp, rows, 2, step)
                store(Turn(0, rows - 1, 2))
                for k in range(2):
                    sp.wait_ge(s_st[k].sem, 16 * (rows // 2))

            @block.gpsimd
            def _(pool):
                pool.wait_ge(s_c, 6)

                def biased(r):
                    slot_wait(pool, s_ld, r)
                    if (r - 2).exists():
                        d_y.wait(pool, r - 2)
                    for v in range(SEGS):
                        last = pool.tensor_tensor(xb[r.step % 2][:, v, :], xt[r.step % 2][:, v, :], bos[:, 1, :], ALU.add)
                    g_xb.mark(last)

                def divide(t):
                    br, j = ur_of(t) // SEGS, t.step % SEGS
                    r = row_of(t)
                    a_av.wait(pool, t)
                    d_rden.wait(pool, t)
                    if ur_of(t) == 0 and (r - 2).exists():
                        t_y.wait(pool, r - 2, "3")
                    to = oT[r.step % 2][br]
                    if br == 0:
                        to = to[:, :, j * P:(j + 1) * P]
                    else:
                        off, half_ = j // 2, j % 2
                        to = to[:].rearrange("p c (k two) -> p c two k", two=2)[:, :, off, half_ * P:(half_ + 1) * P]
                    g_o.mark(pool.tensor_tensor(to, av[:], rden[:], ALU.mult))

                norm.root(pool, first_row)
                norm.root(pool, first_row + 1)
                biased(first_row)

                def step(t):
                    u, r = ur_of(t), row_of(t)
                    if u == 5 and (r + 2).exists(last=rows):
                        norm.root(pool, r + 2)
                    if u == 7 and (r + 1).exists(last=rows):
                        biased(r + 1)
                    divide(t)
                turns(pool, units, 2 * UR, step)

            @block.tensor
            def _(pe):
                pe.wait_ge(s_w, 16 * WEIGHT_DMAS)
                pe.wait_ge(s_c, 6)

                def turn_h(r, j):
                    norm.d_h.wait(pe, r)
                    for v in range(2):
                        for c in range(DC):
                            last = pe.transpose(p_x[:, (c * 2 + v) * P:(c * 2 + v + 1) * P],
                                                h[:, 2 * j + v, c * P:(c + 1) * P], ident[:])
                    t_hT.mark(last, str(j))

                def target(t):
                    u = ur_of(t)
                    return hT[(t.step // UR) % 2], u // SEGS, u % SEGS

                def projected(pe, t):
                    if (t - 1).exists():
                        d_v.wait(pe, t - 1)

                def query(t):
                    x, br, j = target(t)
                    if br == 0 and j == 0:
                        r = row_of(t)
                        a_hT.wait(pe, r, "1")
                        d_hT.wait(pe, r, "1")
                    projected(pe, t)
                    for c in range(DC):
                        last = matmul_split(pe, p_pr[:], [a[:, c, j * P:(j + 1) * P] for a in wq[br]],
                                            [tokens(a[:, c, :], br, 0, S) for a in x], c == 0, c == DC - 1)
                    t_q.mark(last)

                def key(t):
                    x, br, j = target(t)
                    a_q.wait(pe, t)
                    for c in range(DC):
                        last = matmul_split(pe, p_pr[:], [a[:, c, j * P:(j + 1) * P] for a in wk[br]],
                                            [tokens(a[:, c, :], br, 0, S) for a in x], c == 0, c == DC - 1)
                    t_k.mark(last)

                def value(t):
                    x, br, j = target(t)
                    a_k.wait(pe, t)
                    for c in range(DC):
                        last = matmul_split(pe, p_pr[:, 0:D], [tokens(a[:, c, :], br, j * P, P) for a in x],
                                            [a[:, c, :] for a in wv[br]], c == 0, c == DC - 1)
                    t_v.mark(last)

                def scores(t):
                    br, j = ur_of(t) // SEGS, t.step % SEGS
                    if j == 0:
                        a_q.wait(pe, t + (SEGS - 1))
                        a_k.wait(pe, t + (SEGS - 1))
                    for c in range(4):
                        for b in range(4):
                            if c == 0 and (t - 1).exists():
                                a_ex.wait(pe, t - 1, str(b))
                            rr = slice(SLOT * b, SLOT * b + HD)
                            last = pe.matmul(p_s[b][:, c, :], qT[br][rr, c, j * P:(j + 1) * P],
                                             kT[br][rr, c, j * P:(j + 1) * P], start=True, stop=True)
                            if c == 3:
                                t_s.mark(last, str(b))

                def maxima(t):
                    d_max.wait(pe, t, "3")
                    if (t - 1).exists():
                        d_qa.wait(pe, t - 1)
                    for c in range(4):
                        last = pe.transpose(p_m[:, c * P:(c + 1) * P], mpad[:, c, :], ident[:])
                    t_m.mark(last)

                def scores_t(t):
                    br, j = ur_of(t) // SEGS, t.step % SEGS
                    d_qa.wait(pe, t)
                    for c in range(4):
                        for b in range(4):
                            rr = slice(SLOT * b, SLOT * b + HD + 1)
                            last = pe.matmul(p_s[b][:, c, :], kT[br][rr, c, j * P:(j + 1) * P],
                                             qa[rr, c, :], start=True, stop=True)
                            if c == 3:
                                t_st.mark(last, str(b))

                def attend(t):
                    br, j = ur_of(t) // SEGS, t.step % SEGS
                    a_ex.wait(pe, t, "3")
                    d_v.wait(pe, t)
                    if (t - 1).exists():
                        a_av.wait(pe, t - 1)
                    for hd in range(MH):
                        b, c = hd % 4, hd // 4
                        last = pe.matmul(p_av[SLOT * b:SLOT * (b + 1), c * P:(c + 1) * P], va[br][:, j, hd, :],
                                         ex[:, b, c, :], start=True, stop=True)
                    t_av.mark(last)

                def spread(t):
                    a_av.wait(pe, t)
                    self_free(t)
                    t_den.mark(pe.matmul(p_x[:], sel[:], av[:].rearrange("p c n -> p (c n)"), start=True, stop=True))

                def self_free(t):
                    n = t + 1
                    u, r = ur_of(n), row_of(n)
                    if u < 2 and (r + 1).exists(last=rows):
                        d_hT.wait(pe, r + 1, str(u))
                    if OUT_AT <= u < OUT_AT + 4 and (r - 1).exists():
                        d_y.wait(pe, r - 1, str(u - OUT_AT))

                def put_out(r, v):
                    if v == 0:
                        g_o.wait(pe, Turn(r.group, r.step * UR + UR - 1, 2 * UR))
                    for br in range(BR):
                        for c in range(4):
                            last = pe.matmul(p_x[:, 0:D], oT[r.step % 2][br][:, c, v * P:(v + 1) * P], wo[:, br, c, :],
                                             start=br == c == 0, stop=(br, c) == (BR - 1, 3))
                    t_y.mark(last, str(v))

                for j in range(2):
                    if j:
                        d_hT.wait(pe, first_row, "0")
                    turn_h(first_row, j)
                d_hT.wait(pe, first_row, "1")
                for j in range(SEGS):
                    query(first_unit + j)
                    key(first_unit + j)
                    value(first_unit + j)

                def step(t):
                    u, r = ur_of(t), row_of(t)
                    if (t - 2).exists():
                        a_den.wait(pe, t - 2)
                    if u < 2 and (r + 1).exists(last=rows):
                        turn_h(r + 1, u)
                    if OUT_AT <= u < OUT_AT + 4 and (r - 1).exists():
                        put_out(r - 1, u - OUT_AT)
                    ahead = (t + SEGS).exists(last=units)
                    if ahead:
                        query(t + SEGS)
                    scores(t)
                    if (t - 1).exists():
                        attend(t - 1)
                    if ahead:
                        key(t + SEGS)
                    maxima(t)
                    if ahead:
                        value(t + SEGS)
                    if (t - 1).exists():
                        spread(t - 1)
                    scores_t(t)
                turns(pe, units, 2 * UR, step)
                end = first_unit + (units - 1)
                end = Turn(end.group, end.step, 2 * UR)
                attend(end)
                a_den.wait(pe, end - 1)
                spread(end)
                for v in range(4):
                    if v:
                        d_y.wait(pe, first_row + (rows - 1), str(v - 1))
                    put_out(first_row + (rows - 1), v)

            @block.scalar
            def _(act):
                act.wait_ge(s_c, 6)

                def turn_h(r, j):
                    t_hT.wait(act, r, str(j))
                    a_hT.mark(act.copy(hT[r.step % 2][0][:, :, j * 2 * P:(j + 1) * 2 * P],
                                       p_x[:].rearrange("p (c n) -> p c n", c=DC)), str(j))

                def query(t):
                    br, j = ur_of(t) // SEGS, t.step % SEGS
                    t_q.wait(act, t)
                    a_q.mark(act.activation(qT[br][:, j, :], p_pr[:], ACT.Identity, bias=bqs[:, br, j:j + 1], scale=HD ** -0.5))

                def key(t):
                    br, j = ur_of(t) // SEGS, t.step % SEGS
                    t_k.wait(act, t)
                    a_k.mark(act.activation(kT[br][:, j, :], p_pr[:], ACT.Identity, bias=bk1[:, br, j:j + 1]))

                def values(t):
                    t_av.wait(act, t)
                    if (t - 1).exists():
                        g_o.wait(act, t - 1)
                    a_av.mark(act.copy(av[:].rearrange("p c n -> p (c n)"), p_av[:]))

                def spread(t):
                    t_den.wait(act, t)
                    a_den.mark(act.copy(den[:].rearrange("p c n -> p (c n)"), p_x[:]))

                def exps(t):
                    if (t - 1).exists():
                        t_av.wait(act, t - 1)
                    for b in range(4):
                        t_st.wait(act, t, str(b))
                        a_ex.mark(act.activation(ex[:, b, :, :], p_s[b][:], ACT.Exp), str(b))

                for j in range(2):
                    turn_h(first_row, j)
                for j in range(SEGS):
                    query(first_unit + j)
                    key(first_unit + j)

                def step(t):
                    u, r = ur_of(t), row_of(t)
                    if u < 2 and (r + 1).exists(last=rows):
                        turn_h(r + 1, u)
                    ahead = (t + SEGS).exists(last=units)
                    if ahead:
                        query(t + SEGS)
                    if (t - 1).exists():
                        values(t - 1)
                    if ahead:
                        key(t + SEGS)
                    if (t - 1).exists():
                        spread(t - 1)
                    exps(t)
                turns(act, units, 2 * UR, step)
                end = first_unit + (units - 1)
                values(Turn(end.group, end.step, 2 * UR))
                spread(Turn(end.group, end.step, 2 * UR))

            @block.vector
            def _(dve):
                dve.memset(bq[:], 0.0).then_inc(s_z, 1)
                dve.memset(bk[:], 0.0).then_inc(s_z, 1)
                dve.memset(wo[:], 0.0).then_inc(s_z, 1)
                dve.memset(half[:], -0.5).then_inc(s_c, 1)
                dve.memset(mpad[:], 0.0).then_inc(s_c, 1)
                for br in range(BR):
                    dve.memset(va[br][:, :, :, HD:HD + 1], 1.0)
                    last = dve.memset(va[br][:, :, :, HD + 1:], 0.0)
                last.then_inc(s_c, 1)
                dve.wait_ge(s_w, 16 * WEIGHT_DMAS)
                dve.tensor_scalar(bqs[:], bq[:], HD ** -0.5, None, ALU.mult)
                dve.tensor_scalar(bk1[:], bk[:], kone[:, 0:1], None, ALU.add).then_inc(s_c, 1)
                dve.tensor_tensor(bos[:, 0, :], bo[:, 0, :], bo[:, 1, :], ALU.add).then_inc(s_c, 1)
                dve.wait_ge(s_c, 5)
                dve.tensor_scalar(bos[:, 1, :], bos[:, 0, :], BRANCH_WEIGHT, None, ALU.mult).then_inc(s_c, 1)

                def turn_h(r, j):
                    a_hT.wait(dve, r, str(j))
                    x = hT[r.step % 2]
                    cols = slice(j * 2 * P, (j + 1) * 2 * P)
                    d_hT.mark(dve.tensor_tensor(x[1][:, :, cols], p_x[:].rearrange("p (c n) -> p c n", c=DC),
                                                x[0][:, :, cols].bitcast(F32), ALU.subtract), str(j))

                def value(t):
                    br, j = ur_of(t) // SEGS, t.step % SEGS
                    t_v.wait(dve, t)
                    d_v.mark(dve.tensor_tensor(va[br][:, j, :, 0:HD], p_pr[:, 0:D].rearrange("p (h d) -> p h d", h=MH),
                                               bv[:, br, :].rearrange("p (h d) -> p h d", h=MH), ALU.add))

                def maxima(t):
                    if (t - 1).exists():
                        t_m.wait(dve, t - 1)
                    for b in range(4):
                        t_s.wait(dve, t, str(b))
                        d_max.mark(dve.tensor_reduce(mpad[:, :, SLOT * b + HD], p_s[b][:], AX.X, ALU.max,
                                                     negate=True), str(b))

                def invert(t):
                    a_den.wait(dve, t)
                    if (t - 1).exists():
                        g_o.wait(dve, t - 1)
                    d_rden.mark(dve.reciprocal(rden[:], den[:]))

                def augment(t):
                    br, j = ur_of(t) // SEGS, t.step % SEGS
                    t_m.wait(dve, t)
                    if (t - 1).exists():
                        t_st.wait(dve, t - 1, "3")
                    d_qa.mark(dve.tensor_tensor(qa[:], p_m[:].rearrange("p (c n) -> p c n", c=4),
                                                qT[br][:, :, j * P:(j + 1) * P], ALU.add))

                def put_out(r, v):
                    t_y.wait(dve, r, str(v))
                    if v == 0:
                        g_xb.wait(dve, r)
                        if (r - 2).exists():
                            slot_wait(dve, s_st, r - 2)
                    d_y.mark(dve.scalar_tensor_tensor(out=yt[r.step % 2][:, v, :], in0=p_x[:, 0:D], scalar=BRANCH_WEIGHT,
                                                      in1=xb[r.step % 2][:, v, :], op0=ALU.mult, op1=ALU.add), str(v))

                def statistics(r):
                    slot_wait(dve, s_ld, r)
                    norm.statistics(dve, r)

                def scale(r):
                    if (r - 1).exists():
                        t_hT.wait(dve, r - 1, "1")
                    norm.scale(dve, r, h)

                statistics(first_row)
                scale(first_row)
                for j in range(2):
                    turn_h(first_row, j)
                for j in range(SEGS):
                    value(first_unit + j)
                statistics(first_row + 1)
                scale(first_row + 1)

                def step(t):
                    u, r = ur_of(t), row_of(t)
                    if u < 2 and (r + 1).exists(last=rows):
                        turn_h(r + 1, u)
                    if OUT_AT <= u < OUT_AT + 4 and (r - 1).exists():
                        put_out(r - 1, u - OUT_AT)
                    maxima(t)
                    augment(t)
                    if (t + SEGS).exists(last=units):
                        value(t + SEGS)
                    if (t - 1).exists():
                        invert(t - 1)
                    if (r + 2).exists(last=rows):
                        if u == 4:
                            statistics(r + 2)
                        if u == 6:
                            scale(r + 2)
                turns(dve, units, 2 * UR, step)
                invert(Turn(0, units - 1, 2 * UR))
                for v in range(4):
                    put_out(first_row + (rows - 1), v)


UNSEEN = 1e-9
NB = S // P


def batch_attention(nc, name, src, dst, w):
    scratch = {k: nc.dram_tensor(f"{name}_{k}", (P, B * DC * S), F32, kind="Internal").ap() for k in "qkv"}
    project(nc, name + "p", src, scratch, w)
    attend_batch(nc, name + "s", src, dst, scratch, w)


def project(nc, name, src, scratch, w):
    with ExitStack() as ctx:
        m = Memory(nc, ctx, name)
        wq, wk, wv = ([m.sbuf(f"w{n}{k}", DC, D, dt=F32R) for k in "hl"] for n in "qkv")
        with ExitStack() as sub:
            load_split(nc, Memory(nc, sub, name + "w"),
                       [(w[n][c * P:(c + 1) * P, :], t[0][:, c, :], t[1][:, c, :])
                        for n, t in (("bq", wq), ("bk", wk), ("bv", wv)) for c in range(DC)])
        ident, half = m.sbuf("ident", P), m.sbuf("half", 1)
        xt = [m.sbuf(f"xt{k}", NB, D) for k in range(4)]
        h = m.sbuf("h", NB, D)
        hT = [[m.sbuf(f"hT{r}{k}", DC, S, dt=F32R) for k in "hl"] for r in range(2)]
        qT = [m.sbuf(f"qT{k}", DC, S) for k in range(2)]
        kT = [m.sbuf(f"kT{k}", DC, S) for k in range(2)]
        vs = [m.sbuf(f"vs{k}", NB, D) for k in range(2)]
        p_tr, p_q, p_k, p_v = (m.psum(k, DC, S) for k in ("p_tr", "p_q", "p_k", "p_v"))
        s_w, s_c = m.sem("s_w"), m.sem("s_c")
        s_ld = [m.track(f"s_ld{k}", inc=16) for k in range(4)]
        s_q, s_k, s_v = ([m.track(f"s_{n}{k}", inc=16) for k in range(2)] for n in "qkv")
        norm = Norm(m, NB, lambda t: xt[t.step % 4], half)
        t_hT, a_hT, d_hT = m.track("t_hT"), m.track("a_hT"), m.track("d_hT")
        t_q, t_k, t_v = m.track("t_q"), m.track("t_k"), m.track("t_v")
        a_q, a_k, d_v = m.track("a_q"), m.track("a_k"), m.track("d_v")
        count, unroll = B, 4
        first = Turn(0, 0, unroll)

        with nc.Block() as block:
            @block.sync
            def _(sp):
                sp.dma_start(ident[:], w["ident"]).then_inc(s_w, 16)

                def load(t):
                    sp.dma_start(xt[t.step % 4][:], row_tiles(src, t)).then_inc(s_ld[t.step % 4].sem, 16)

                for n in range(3):
                    load(first + n)

                def step(t):
                    if (t + 3).exists(last=count):
                        if (t - 1).exists():
                            norm.d_h.wait(sp, t - 1)
                        load(t + 3)
                    cols = bass.ds(t.times(DC * S, 0), DC * S)
                    for n, written, buf, sems in (("q", a_q, qT, s_q), ("k", a_k, kT, s_k), ("v", d_v, vs, s_v)):
                        written.wait(sp, t)
                        sp.dma_start(scratch[n][:, cols], buf[t.step % 2][:].rearrange("p a b -> p (a b)")
                                     ).then_inc(sems[t.step % 2].sem, 16)
                turns(sp, count, unroll, step)
                for k in range(2):
                    for sems in (s_q, s_k, s_v):
                        sp.wait_ge(sems[k].sem, 16 * (count // 2))

            @block.gpsimd
            def _(pool):
                pool.wait_ge(s_c, 1)
                norm.root(pool, first)

                def step(t):
                    if (t + 1).exists(last=count):
                        norm.root(pool, t + 1)
                turns(pool, count, unroll, step)

            @block.tensor
            def _(pe):
                pe.wait_ge(s_w, 16)

                def turn_h(t):
                    norm.d_h.wait(pe, t)
                    if (t - 1).exists():
                        d_hT.wait(pe, t - 1)
                    for v in range(NB):
                        for c in range(DC):
                            last = pe.transpose(p_tr[:, c, v * P:(v + 1) * P], h[:, v, c * P:(c + 1) * P], ident[:])
                    t_hT.mark(last)

                turn_h(first)

                def step(t):
                    x = hT[t.step % 2]
                    a_hT.wait(pe, t)
                    d_hT.wait(pe, t)
                    if (t - 1).exists():
                        a_q.wait(pe, t - 1)
                    for i in range(DC):
                        for c in range(DC):
                            last = matmul_split(pe, p_q[:, i, :], [a[:, c, i * P:(i + 1) * P] for a in wq],
                                                [a[:, c, :] for a in x], c == 0, c == DC - 1)
                    t_q.mark(last)
                    if (t - 1).exists():
                        a_k.wait(pe, t - 1)
                    for i in range(DC):
                        for parity in range(2):
                            for c in range(DC):
                                last = matmul_split(
                                    pe, p_k[:, i, parity * D:(parity + 1) * D],
                                    [a[:, c, :].rearrange("p (k two) -> p two k", two=2)[:, parity, i * P:(i + 1) * P]
                                     for a in x],
                                    [a[:, c, :] for a in wk], c == 0, c == DC - 1)
                    t_k.mark(last)
                    if (t + 1).exists(last=count):
                        turn_h(t + 1)
                    if (t - 1).exists():
                        d_v.wait(pe, t - 1)
                    for v in range(NB):
                        for c in range(DC):
                            last = matmul_split(pe, p_v[:].rearrange("p c s -> p (c s)")[:, v * D:(v + 1) * D],
                                                [a[:, c, v * P:(v + 1) * P] for a in x],
                                                [a[:, c, :] for a in wv], c == 0, c == DC - 1)
                    t_v.mark(last)
                turns(pe, count, unroll, step)

            @block.scalar
            def _(act):
                def turned(t):
                    t_hT.wait(act, t)
                    if (t - 2).exists():
                        t_v.wait(act, t - 2)
                    a_hT.mark(act.copy(hT[t.step % 2][0][:], p_tr[:]))

                turned(first)

                def step(t):
                    for made, out, p, buf, stored in ((t_q, a_q, p_q, qT, s_q), (t_k, a_k, p_k, kT, s_k)):
                        made.wait(act, t)
                        if (t - 2).exists():
                            slot_wait(act, stored, t - 2)
                        out.mark(act.copy(buf[t.step % 2][:], p[:]))
                    if (t + 1).exists(last=count):
                        turned(t + 1)
                turns(act, count, unroll, step)

            @block.vector
            def _(dve):
                dve.memset(half[:], -0.5).then_inc(s_c, 1)

                def front(t):
                    slot_wait(dve, s_ld, t)
                    norm.statistics(dve, t)
                    if (t - 1).exists():
                        t_hT.wait(dve, t - 1)
                    norm.scale(dve, t, h)

                def turned(t):
                    a_hT.wait(dve, t)
                    x = hT[t.step % 2]
                    d_hT.mark(dve.tensor_tensor(x[1][:], p_tr[:], x[0][:].bitcast(F32), ALU.subtract))

                front(first)
                turned(first)

                def step(t):
                    if (t + 1).exists(last=count):
                        front(t + 1)
                        turned(t + 1)
                    t_v.wait(dve, t)
                    if (t - 2).exists():
                        slot_wait(dve, s_v, t - 2)
                    d_v.mark(dve.tensor_copy(vs[t.step % 2][:].rearrange("p v d -> p (v d)"),
                                             p_v[:].rearrange("p c s -> p (c s)")))
                turns(dve, count, unroll, step)


def attend_batch(nc, name, src, dst, scratch, w):
    with ExitStack() as ctx:
        m = Memory(nc, ctx, name)
        G, GB = 8, 2
        RING = 4
        k_all = m.sbuf("k_all", NB, B, DC, P)
        v_all = m.sbuf("v_all", NB, B, D)
        q_blk = [m.sbuf(f"q_blk{k}", B, DC, P) for k in range(2)]
        at = [m.sbuf(f"at{j}", B, P) for j in range(NB)]
        mx, sm, rc, rt = (m.sbuf(k, P) for k in ("mx", "sm", "rc", "rt"))
        tri, fill, unseen = (m.sbuf(k, P) for k in ("tri", "fill", "unseen"))
        xt = [m.sbuf(f"xt{k}", GB, D) for k in range(2)]
        yt = [m.sbuf(f"yt{k}", GB, D) for k in range(2)]
        p_s = m.psum("p_s", B, P)
        p_o = [m.psum(f"p_o{k}", GB, D) for k in range(RING)]

        s_c, s_z = m.sem("s_c"), m.sem("s_z")
        s_k, s_v = ([m.sem(f"s_{n}{j}") for j in range(NB)] for n in "kv")
        s_q, s_x, s_y = ([m.sem(f"s_{n}{k}") for k in range(2)] for n in "qxy")
        banks = [str(b) for b in range(4)]
        t_s, d_sub, a_e = (m.track(k, *banks) for k in ("t_s", "d_sub", "a_e"))
        d_mx, d_w = m.track("d_mx"), m.track("d_w", "sum", "rc", "mul")
        g_w = m.track("g_w")
        d_diag, g_diag = m.track("d_diag", "rt", "fill"), m.track("g_diag")
        t_o, d_y = m.track("t_o"), m.track("d_y")
        blocks = [(qb, jb) for qb in range(NB) for jb in range(qb + 1)]
        at_ = lambda n: Turn(n, 0, 1)
        last_of = [(qb + 1) * (qb + 2) // 2 - 1 for qb in range(NB)]
        HB = B // 2

        def rows_of(a, qb, g):
            return a.rearrange("(b s) d -> s b d", b=B)[qb * P:(qb + 1) * P, g * GB:(g + 1) * GB, :]

        with nc.Block() as block:
            @block.sync
            def _(sp):
                def load_q(qb):
                    sp.dma_start(q_blk[qb % 2][:].rearrange("p b c s -> p (b c) s"),
                                 scratch["q"].rearrange("p (a s) -> p a s", s=S)[:, :, qb * P:(qb + 1) * P]
                                 ).then_inc(s_q[qb % 2], 16)

                def load_k(jb):
                    sp.dma_start(k_all[:, jb].rearrange("p b c s -> p (b c) s"),
                                 scratch["k"].rearrange("p (a s) -> p a s", s=S)[:, :, jb * P:(jb + 1) * P]
                                 ).then_inc(s_k[jb], 16)

                def load_v(jb):
                    sp.dma_start(v_all[:, jb], scratch["v"].rearrange("p (b v d) -> p b v d", b=B, d=D)[:, :, jb, :]
                                 ).then_inc(s_v[jb], 16)

                def load_x(n):
                    sp.dma_start(xt[n % 2][:], rows_of(src, n // G, n % G)).then_inc(s_x[n % 2], 16)

                load_k(0)
                load_q(0)
                for t, k in ((tri, "tri"), (fill, "fill")):
                    sp.dma_start(t[:], w[k]).then_inc(s_c, 16)
                for jb in range(NB):
                    load_v(jb)
                load_x(0)
                load_x(1)
                load_q(1)
                for jb in range(1, NB):
                    load_k(jb)
                for n in range(NB * G):
                    qb = n // G
                    if n % G == 0 and 1 <= qb < NB - 1:
                        t_s.wait(sp, at_(last_of[qb - 1]))
                        load_q(qb + 1)
                    d_y.wait(sp, at_(n))
                    sp.dma_start(rows_of(dst, qb, n % G), yt[n % 2][:]).then_inc(s_y[n % 2], 16)
                    if n + 2 < NB * G:
                        load_x(n + 2)
                for k in range(2):
                    sp.wait_ge(s_y[k], 16 * (NB * G // 2))

            @block.tensor
            def _(pe):
                pe.wait_ge(s_z, 1)

                def scores(n):
                    qb, jb = blocks[n]
                    if jb == 0:
                        pe.wait_ge(s_q[qb % 2], 16 * (qb // 2 + 1))
                    if jb == qb:
                        pe.wait_ge(s_k[jb], 16)
                    for b in range(B):
                        if b % 4 == 0 and n:
                            d_sub.wait(pe, at_(n - 1), str(b // 4))
                        for c in range(DC):
                            last = pe.matmul(p_s[:, b, :], k_all[:, jb, b, c, :], q_blk[qb % 2][:, b, c, :],
                                             start=c == 0, stop=c == DC - 1)
                        if b % 4 == 3:
                            t_s.mark(last, str(b // 4))

                def outputs(qb):
                    d_w.wait(pe, at_(last_of[qb]), "mul")
                    g_w.wait(pe, at_(last_of[qb]))
                    d_diag.wait(pe, at_(qb), "fill")
                    g_diag.wait(pe, at_(qb))
                    if qb == 0:
                        for jb in range(NB):
                            pe.wait_ge(s_v[jb], 16)
                    for g in range(G):
                        n = qb * G + g
                        if n >= RING:
                            d_y.wait(pe, at_(n - RING))
                        for i in range(GB):
                            b = g * GB + i
                            for jb in range(NB):
                                lhs = at[jb][:, b, :] if jb <= qb else unseen[:]
                                last = pe.matmul(p_o[n % RING][:, i, :], lhs, v_all[:, jb, b, :],
                                                 start=jb == 0, stop=jb == NB - 1)
                        t_o.mark(last)

                for n, (qb, jb) in enumerate(blocks):
                    scores(n)
                    if jb == qb:
                        outputs(qb)

            @block.scalar
            def _(act):
                for n, (qb, jb) in enumerate(blocks):
                    for k in range(4):
                        d_sub.wait(act, at_(n), str(k))
                        x = at[jb][:, 4 * k:4 * k + 4, :]
                        a_e.mark(act.activation(x, x, ACT.Exp, scale=D ** -0.5), str(k))

            @block.gpsimd
            def _(pool):
                pool.wait_ge(s_c, 32)
                for n, (qb, jb) in enumerate(blocks):
                    x, r = at[jb][:, HB:, :], rt if jb == qb else rc
                    d_w.wait(pool, at_(n), "rc")
                    if jb == qb:
                        d_diag.wait(pool, at_(qb), "rt")
                    g_w.mark(pool.tensor_tensor(x, x, r[:].unsqueeze(1).to_broadcast([P, HB, P]), ALU.mult))
                    if jb == qb:
                        g_w.wait(pool, at_(n))
                        g_diag.mark(pool.tensor_tensor(x, x, fill[:].unsqueeze(1).to_broadcast([P, HB, P]), ALU.add))

            @block.vector
            def _(dve):
                dve.memset(unseen[:], UNSEEN).then_inc(s_z, 1)
                dve.wait_ge(s_c, 32)

                def output(n):
                    t_o.wait(dve, at_(n))
                    dve.wait_ge(s_x[n % 2], 16 * (n // 2 + 1))
                    if n >= 2:
                        dve.wait_ge(s_y[n % 2], 16 * (n // 2))
                    d_y.mark(dve.tensor_tensor(yt[n % 2][:], p_o[n % RING][:], xt[n % 2][:], ALU.add))

                for n, (qb, jb) in enumerate(blocks):
                    t_s.wait(dve, at_(n))
                    if n:
                        d_sub.wait(dve, at_(n - 1))
                    d_mx.mark(dve.tensor_reduce(mx[:], p_s[:].rearrange("p b s -> p s b"), AX.X, ALU.max))
                    d_mx.wait(dve, at_(n))
                    if jb < qb and qb:
                        t_o.wait(dve, at_(qb * G - 1))
                    for k in range(4):
                        d_sub.mark(dve.tensor_tensor(at[jb][:, 4 * k:4 * k + 4, :], p_s[:, 4 * k:4 * k + 4, :],
                                                     mx[:].unsqueeze(1).to_broadcast([P, 4, P]), ALU.subtract), str(k))
                    a_e.wait(dve, at_(n))
                    if n:
                        d_w.wait(dve, at_(n - 1), "mul")
                        g_w.wait(dve, at_(n - 1))
                    x = at[jb][:].rearrange("p b s -> p s b")
                    d_w.mark(dve.tensor_reduce(sm[:], x, AX.X, ALU.add), "sum")
                    d_w.wait(dve, at_(n), "sum")
                    d_w.mark(dve.reciprocal(rc[:], sm[:]), "rc")
                    d_w.wait(dve, at_(n), "rc")
                    x, r = at[jb][:, 0:HB, :], rc
                    if jb == qb:
                        d_diag.mark(dve.tensor_tensor(rt[:], rc[:], tri[:], ALU.mult), "rt")
                        d_diag.wait(dve, at_(qb), "rt")
                        r = rt
                    d_w.mark(dve.tensor_tensor(x, x, r[:].unsqueeze(1).to_broadcast([P, HB, P]), ALU.mult), "mul")
                    if jb == qb:
                        d_w.wait(dve, at_(n), "mul")
                        d_diag.mark(dve.tensor_tensor(x, x, fill[:].unsqueeze(1).to_broadcast([P, HB, P]), ALU.add), "fill")
                        for g in range(G):
                            output(qb * G + g)


def clear_semaphores(nc):
    used = sorted(nc.released_uncleared_semaphores)
    assert set(range(used[0], used[-1] + 1)) <= set(nc.free_semaphores)
    with nc.Block() as block:
        @block.gpsimd
        def _(pool):
            pool.sem_clear(range(used[0], used[-1] + 1))


def macaron(nc, out, x, w):
    stages = [(expert_ffn, "f1"), (dilated_attention, "a1"), (expert_ffn, "f2"),
              (channel_mix, "c1"), (batch_attention, "b1"), (channel_mix, "c2")]
    src = x
    for n, (stage, name) in enumerate(stages):
        dst = out if n == len(stages) - 1 else nc.dram_tensor(f"x_{name}", (N, D), F32, kind="Internal").ap()
        stage(nc, name, src, dst, w)
        src = dst
        if n < len(stages) - 1:
            clear_semaphores(nc)


def layouts(i):
    turn = lambda a, *axes: np.ascontiguousarray(np.transpose(a, axes or None))
    heads = lambda a: turn(a.reshape(BR, 4, 4, HD), 0, 2, 3, 1)
    qkv, bias = i["L0_attn_Wqkv"][:BR], i["L0_attn_bqkv"][:BR]
    tri = np.triu(np.ones((P, P), np.float32))
    kone = np.zeros((P, 1), np.float32)
    kone[HD::SLOT] = 1
    sel = np.kron(np.eye(4, dtype=np.float32), np.ones((SLOT, SLOT), np.float32)) * kone
    return {
        "ident": np.eye(P, dtype=np.float32), "tri": tri, "fill": np.float32(UNSEEN) * (1 - tri), "kone": kone, "sel": sel,
        "wq": i["L0_ffn_W_q"], "up_embed": i["L0_ffn_up_embed"], "wdn": turn(i["L0_ffn_W_down"]),
        "keys": turn(i["L0_ffn_keys"], 2, 0, 3, 1).reshape(2 * HEADS, KEYS, KEYS),
        "wdown": turn(i["L0_ffn_down_embed"]), "wup": turn(i["L0_ffn_W_up"]),
        "aq": turn(qkv[:, :D], 0, 2, 1), "ak": turn(qkv[:, D:2 * D], 0, 2, 1), "av": turn(qkv[:, 2 * D:], 0, 2, 1),
        "abq": heads(bias[:, :D]), "abk": heads(bias[:, D:2 * D]), "abv": np.ascontiguousarray(bias[:, 2 * D:]),
        "ao": turn(i["L0_attn_Wout"][:BR], 0, 2, 1), "abo": np.ascontiguousarray(i["L0_attn_bout"][:BR]),
        "bq": turn(i["L1_attn_Wq"]), "bk": turn(i["L1_attn_Wk"]), "bv": turn(i["L1_attn_Wv"]),
        "wr": turn(i["L1_ffn_W_r"]), "wk": turn(i["L1_ffn_W_k"]), "wv": turn(i["L1_ffn_W_v"]),
        "mu_r": i["L1_ffn_mu_r"], "mu_k": i["L1_ffn_mu_k"],
    }


def kernel(**inputs):
    from concourse import bacc
    from concourse.bass_utils import run_bass_kernel_spmd

    inputs = {k: np.asarray(v) for k, v in inputs.items()}
    arrays = {"x": np.ascontiguousarray(inputs["L0_attn_x"]).reshape(N, D)}
    arrays.update({k: np.ascontiguousarray(v) for k, v in layouts(inputs).items()})
    nc = bacc.Bacc("TRN2", target_bir_lowering=False, num_devices=1)
    w = {k: nc.dram_tensor(k, a.shape, F32, kind="ExternalInput").ap() for k, a in arrays.items()}
    out = nc.dram_tensor("out", (N, D), F32, kind="ExternalOutput").ap()
    macaron(nc, out, w.pop("x"), w)
    result = run_bass_kernel_spmd(nc, [arrays], core_ids=[0])
    return result.results[0]["out"].reshape(B, S, D)
```

```python
from contextlib import ExitStack

import numpy as np
import concourse.bass as bass
from concourse import mybir
from concourse.alu_op_type import AluOpType as ALU

ACT = mybir.ActivationFunctionType
AX = mybir.AxisListType
F32 = mybir.dt.float32
F32R = mybir.dt.float32r

P = 128
B, S, D = 16, 512, 256
N = B * S
DC = D // P
EPS = 1e-5


class Turn:

    def __init__(self, group, step, unroll):
        self.group, self.step, self.unroll = group + step // unroll if step // unroll else group, step % unroll, unroll

    def __add__(self, k):
        return Turn(self.group, self.step + k, self.unroll)

    def __sub__(self, k):
        return self + (-k)

    def exists(self, first=0, last=None):
        if not isinstance(self.group, int):
            return True
        n = self.group * self.unroll + self.step
        return n >= first and (last is None or n < last)

    def times(self, per, plus):
        return self.group * (self.unroll * per) + (self.step * per + plus)

    def rows(self, size, offset=0, count=None):
        return bass.ds(self.times(size, offset), size if count is None else count)


class Track:

    def __init__(self, sem, *marks, inc=1):
        self.sem, self.marks, self.inc = sem, marks, inc

    def mark(self, instruction, name=None):
        assert name is None or name in self.marks
        instruction.then_inc(self.sem, self.inc)

    def wait(self, engine, turn, name=None, alone=False):
        at = self.marks.index(name) + 1 if name else len(self.marks)
        n = len(self.marks) * self.inc
        engine.wait_ge(self.sem, turn.times(n, at * self.inc))
        if alone:
            engine.nop(nofuse=True)


def turns(engine, count, unroll, step):
    groups = count // unroll
    assert groups * unroll == count and groups >= 2
    for u in range(unroll):
        step(Turn(0, u, unroll))
    if groups > 2:
        with engine.Fori(1, groups - 1) as g:
            for u in range(unroll):
                step(Turn(g, u, unroll))
    for u in range(unroll):
        step(Turn(groups - 1, u, unroll))


class Memory:

    def __init__(self, nc, ctx, name):
        self.nc, self.ctx, self.name = nc, ctx, name

    def sbuf(self, name, *shape, dt=F32):
        return self.ctx.enter_context(self.nc.sbuf_tensor(f"{self.name}_{name}", [P, *shape], dt))

    def psum(self, name, *shape):
        return self.ctx.enter_context(self.nc.psum_tensor(f"{self.name}_{name}", [P, *shape], F32))

    def sem(self, name):
        return self.ctx.enter_context(self.nc.semaphore(f"{self.name}_{name}"))

    def track(self, name, *marks, inc=1):
        return Track(self.sem(name), *(marks or (name,)), inc=inc)


def matmul_split(pe, out, lhs, rhs, start, stop):
    (lh, ll), (rh, rl) = lhs, rhs
    pe.matmul(out, lh, rl, start=start, stop=False)
    pe.matmul(out, ll, rh, start=False, stop=False)
    return pe.matmul(out, lh, rh, start=False, stop=stop)


class SplitLoad:

    STAGES = 4

    def __init__(self, m, loads):
        self.loads = loads
        self.stage = [m.sbuf(f"stage{k}", 1024) for k in range(self.STAGES)]
        self.s_ld = [m.sem(f"s_stage{k}") for k in range(self.STAGES)]
        self.s_zero, self.s_hi, self.s_lo = m.sem("s_zero"), m.sem("s_hi"), m.sem("s_lo")

    def raw(self, n):
        return self.stage[n % self.STAGES][:, 0:self.loads[n][1].shape[1]]

    def sync(self, sp):
        sp.wait_ge(self.s_zero, self.STAGES)
        for n, (src, hi, lo, heads) in enumerate(self.loads):
            if n >= self.STAGES:
                sp.wait_ge(self.s_lo, n - self.STAGES + 1)
            raw = self.raw(n)
            if heads:
                raw = raw.rearrange("p (h s) -> p h s", s=heads[1])[:, :, 0:heads[0]]
                src = src.rearrange("p (h d) -> p h d", d=heads[0])
            sp.dma_start(raw, src).then_inc(self.s_ld[n % self.STAGES], 16)

    def scalar(self, act):
        for n, (src, hi, lo, heads) in enumerate(self.loads):
            act.wait_ge(self.s_ld[n % self.STAGES], 16 * (n // self.STAGES + 1))
            act.copy(hi, self.raw(n)).then_inc(self.s_hi, 1)

    def vector(self, dve):
        for k in range(self.STAGES):
            dve.memset(self.stage[k][:], 0.0).then_inc(self.s_zero, 1)
        for n, (src, hi, lo, heads) in enumerate(self.loads):
            dve.wait_ge(self.s_ld[n % self.STAGES], 16 * (n // self.STAGES + 1))
            dve.wait_ge(self.s_hi, n + 1)
            dve.tensor_tensor(lo, self.raw(n), hi.bitcast(F32), ALU.subtract).then_inc(self.s_lo, 1)


def load_split(nc, m, loads):
    split = SplitLoad(m, loads)
    with nc.Block() as block:
        block.sync(split.sync)
        block.scalar(split.scalar)
        block.vector(split.vector)


class Norm:

    def __init__(self, m, tiles, x_of, half):
        self.tiles, self.x_of, self.half = tiles, x_of, half
        self.bs, self.mv = m.sbuf("bs", 2, tiles, 6), m.sbuf("mv", 2, tiles, 2)
        self.ve, self.rstd = m.sbuf("ve", 2, tiles), m.sbuf("rstd", 2, tiles)
        self.d_ln = m.track("d_ln", "bn", "mv")
        self.g_ln = m.track("g_ln", "ve", "rstd")
        self.d_h = m.track("d_h")

    def statistics(self, dve, t):
        k, x = t.step % 2, self.x_of(t)
        for v in range(self.tiles):
            last = dve.bn_stats(self.bs[:, k, v, :], x[:, v, :])
        self.d_ln.mark(last, "bn")
        self.d_ln.wait(dve, t, "bn", alone=True)
        for v in range(self.tiles):
            last = dve.bn_aggr(self.mv[:, k, v, :], self.bs[:, k, v, :])
        self.d_ln.mark(last, "mv")

    def root(self, pool, t):
        k = t.step % 2
        self.d_ln.wait(pool, t, "mv", alone=True)
        self.g_ln.mark(pool.tensor_scalar(self.ve[:, k, :], self.mv[:, k, :, 1], EPS, None, ALU.add), "ve")
        self.g_ln.wait(pool, t, "ve")
        self.g_ln.mark(pool.tensor_tensor(self.rstd[:, k, :], self.ve[:, k, :],
                                          self.half[:, 0:1].to_broadcast([P, self.tiles]), ALU.pow), "rstd")

    def scale(self, dve, t, h):
        k, x = t.step % 2, self.x_of(t)
        self.g_ln.wait(dve, t, "rstd")
        for v in range(self.tiles):
            last = dve.tensor_scalar(h[:, v, :], x[:, v, :], self.mv[:, k, v, 0:1],
                                     self.rstd[:, k, v:v + 1], ALU.subtract, ALU.mult)
        self.d_h.mark(last)


def slot_wait(e, tracks, t):
    k = len(tracks)
    e.wait_ge(tracks[t.step % k].sem, t.group * (16 * (t.unroll // k)) + 16 * (t.step // k + 1))


def row_tiles(a, t):
    return a[t.rows(S), :].rearrange("(v p) d -> p v d", p=P)


HEADS, KEYS, TOP = 4, 64, 8
EXPERTS, HID = 1024, 1024
XROWS = EXPERTS // KEYS
GRID = EXPERTS + TOP * TOP
V = 2
EC = EXPERTS // P


def expert_ffn(nc, name, src, dst, w):
    with ExitStack() as ctx:
        m = Memory(nc, ctx, name)
        ws = [m.sbuf(f"ws{k}", DC, 2 * HEADS * KEYS, dt=F32R) for k in "hl"]
        wdown = [m.sbuf(f"wdown{k}", DC, EXPERTS, dt=F32R) for k in "hl"]
        wup = [m.sbuf(f"wup{k}", DC, HID, dt=F32R) for k in "hl"]
        eup = m.sbuf("eup", EC, D)
        wdn = m.sbuf("wdn", HID // P, D)
        ident, half = m.sbuf("ident", P), m.sbuf("half", 1)
        with ExitStack() as sub:
            ms = Memory(nc, sub, name + "w")
            fold = ms.sbuf("fold", DC, 2 * HEADS * KEYS)
            s_q, s_late, s_z, s_f, s_fc = ms.sem("s_q"), ms.sem("s_late"), ms.sem("s_z"), ms.sem("s_f"), ms.sem("s_fc")
            wq = ms.sbuf("wq", 4, D)
            kt = ms.sbuf("kt", 4, P)
            pf = ms.psum("pf", DC, 2 * HEADS * KEYS)
            split = SplitLoad(ms, [(w[n][c * P:(c + 1) * P, :], t[0][:, c, :], t[1][:, c, :], None)
                                   for n, t in (("wdown", wdown), ("wup", wup)) for c in range(DC)])
            with nc.Block() as block:
                block.scalar(split.scalar)

                @block.vector
                def _(dve):
                    dve.memset(kt[:], 0.0).then_inc(s_z, 1)
                    dve.memset(half[:], -0.5).then_inc(s_z, 1)
                    split.vector(dve)
                    dve.wait_ge(s_f, 1)
                    dve.tensor_copy(fold[:], pf[:]).then_inc(s_fc, 1)
                    dve.wait_ge(s_fc, 1)
                    dve.tensor_copy(ws[0][:], fold[:]).then_inc(s_fc, 1)
                    dve.wait_ge(s_fc, 2)
                    dve.tensor_tensor(ws[1][:], fold[:], ws[0][:].bitcast(F32), ALU.subtract).then_inc(s_fc, 1)

                @block.sync
                def _(sp):
                    sp.dma_start(wq[:], w["wq"].rearrange("(e p) c -> p e c", p=P)).then_inc(s_q, 16)
                    sp.wait_ge(s_z, 1)
                    for g in range(2 * HEADS):
                        r = (g % 2) * KEYS
                        sp.dma_start(kt[r:r + KEYS, g // 2, r:r + KEYS], w["keys"][g]).then_inc(s_q, 16)
                    split.sync(sp)
                    sp.dma_start(ident[:], w["ident"]).then_inc(s_late, 16)
                    sp.dma_start(eup[:], w["up_embed"].rearrange("(e p) d -> p e d", p=P)).then_inc(s_late, 16)
                    sp.dma_start(wdn[:], w["wdn"].rearrange("(e p) d -> p e d", p=P)).then_inc(s_late, 16)
                    sp.wait_ge(s_late, 16 * 3)

                @block.tensor
                def _(pe):
                    pe.wait_ge(s_q, 16 * 9)
                    for c in range(DC):
                        for e in range(4):
                            mm = pe.matmul(pf[:, c, e * P:(e + 1) * P], wq[:, e, c * P:(c + 1) * P],
                                           kt[:, e, :], start=True, stop=True)
                    mm.then_inc(s_f, 1)

        xt = [m.sbuf(f"xt{k}", V, D) for k in range(4)]
        yt = [m.sbuf(f"yt{k}", V, D) for k in range(2)]
        h = m.sbuf("h", V, D)
        hT = [[m.sbuf(f"hT{r}{k}", DC, V * P, dt=F32R) for k in "hl"] for r in range(2)]
        sim = m.sbuf("sim", V, 2 * HEADS * KEYS)
        tx, ty, tc, tp, tm, te = (m.sbuf(k, V, HEADS, TOP) for k in ("tx", "ty", "tc", "tp", "tm", "te"))
        cand = m.sbuf("cand", V, HEADS, TOP * TOP)
        negm, z, rz = (m.sbuf(k, V, HEADS) for k in ("negm", "z", "rz"))
        p_last = m.sbuf("p_last", V)
        grid = [m.sbuf(f"grid{v}", HEADS, GRID) for v in range(V)]
        q = [m.sbuf(f"q{v}", HEADS, GRID) for v in range(V)]
        clamped = m.sbuf("clamped", V)
        wT = [m.sbuf(f"wT{v}", EC, P) for v in range(V)]
        hs = m.sbuf("hs", HID // P, V * P)

        p_tr, p_sim, p_out, p_h = (m.psum(k, 512) for k in ("p_tr", "p_sim", "p_out", "p_h"))
        p_hid = (p_h, p_tr)
        p_y = (p_out[:, 0:D], p_h[:, 0:D])
        p_dot, p_wT = m.psum("p_dot", EXPERTS), m.psum("p_wT", EC, P)

        s_ld = [m.track(f"s_ld{k}", inc=16) for k in range(4)]
        s_st = [m.track(f"s_st{k}", inc=16) for k in range(2)]
        norm = Norm(m, V, lambda t: xt[t.step % 4], half)
        t_hT = m.track("t_hT")
        a_hT, d_hT = m.track("a_hT"), m.track("d_hT")
        t_sim = m.track("t_sim", "0", "1")
        a_sim = m.track("a_sim", "0", "1")
        d_top = m.track("d_top", "maxes", "cand", "clamped pairs", "best", "negm", "tm")
        a_te = m.track("a_te")
        d_z = m.track("d_z", "z", "rz")
        g_grid = m.track("g_grid", "0", "1")
        t_dot = m.track("t_dot", "0", "1")
        d_last = m.track("d_last", "0", "1")
        d_mask = m.track("d_mask", "0", "1")
        a_exp = m.track("a_exp", "0", "1")
        d_mul = m.track("d_mul", "0", "1")
        a_silu = m.track("a_silu", "0", "1")
        d_clamp = m.track("d_clamp", "sum0", "add0", "sum1", "add1")
        t_hid = m.track("t_hid", *(str(k) for k in range(4)))
        a_hid = m.track("a_hid", *(str(k) for k in range(4)))
        t_wT = m.track("t_wT", "0", "1")
        a_wT = m.track("a_wT", "0", "1")
        t_out = m.track("t_out", "0", "1")
        d_out = m.track("d_out", "0", "1")

        count, unroll = N // (V * P), 4
        rows = lambda a, t: a[t.rows(V * P), :].rearrange("(v p) d -> p v d", p=P)

        with nc.Block() as block:
            @block.sync
            def _(sp):
                def load(t):
                    k = t.step % 4
                    sp.dma_start(xt[k][:], rows(src, t)).then_inc(s_ld[k].sem, 16)

                def store(t):
                    k = t.step % 2
                    d_out.wait(sp, t, "1")
                    sp.dma_start(rows(dst, t), yt[k][:]).then_inc(s_st[k].sem, 16)

                for n in range(3):
                    load(Turn(0, n, unroll))

                def step(t):
                    if (t - 1).exists():
                        store(t - 1)
                    if (t + 3).exists(last=count):
                        load(t + 3)
                turns(sp, count, unroll, step)
                store(Turn(0, count - 1, unroll))
                for k in range(2):
                    sp.wait_ge(s_st[k].sem, 16 * (count // 2))

            @block.gpsimd
            def _(pool):
                def scores(t, v):
                    a_sim.wait(pool, t, str(v))
                    if (t - 1).exists():
                        d_mul.wait(pool, t - 1, str(v))
                    sx = sim[:, v, 0:HEADS * KEYS].rearrange("p (h k) -> p h k", h=HEADS)[:, :, 0:XROWS]
                    sy = sim[:, v, HEADS * KEYS:].rearrange("p (h k) -> p h k", h=HEADS)
                    for hd in range(HEADS):
                        last = pool.tensor_tensor(
                            grid[v][:, hd, 0:EXPERTS].rearrange("p (i j) -> p i j", i=XROWS),
                            sx[:, hd, :].unsqueeze(2).to_broadcast([P, XROWS, KEYS]),
                            sy[:, hd, :].unsqueeze(1).to_broadcast([P, XROWS, KEYS]), ALU.add)
                    g_grid.mark(last, str(v))

                norm.root(pool, Turn(0, 0, unroll))
                norm.root(pool, Turn(0, 1, unroll))

                def step(t):
                    scores(t, 0)
                    scores(t, 1)
                    if (t + 2).exists(last=count):
                        norm.root(pool, t + 2)
                turns(pool, count, unroll, step)

            @block.tensor
            def _(pe):
                def turn_h(t):
                    norm.d_h.wait(pe, t)
                    if (t - 1).exists():
                        d_hT.wait(pe, t - 1)
                    if (t - 2).exists():
                        a_hid.wait(pe, t - 2, "3")
                    for v in range(V):
                        for c in range(DC):
                            last = pe.transpose(p_tr[:, (c * V + v) * P:(c * V + v + 1) * P],
                                                h[:, v, c * P:(c + 1) * P], ident[:])
                    t_hT.mark(last)

                def similar(t, v):
                    if v == 0:
                        a_hT.wait(pe, t)
                        d_hT.wait(pe, t)
                    if v:
                        a_sim.wait(pe, t, "0")
                    elif (t - 1).exists():
                        a_sim.wait(pe, t - 1, "1")
                    for c in range(DC):
                        last = matmul_split(pe, p_sim[:], [x[:, c, v * P:(v + 1) * P] for x in hT[t.step % 2]],
                                            [x[:, c, :] for x in ws], c == 0, c == DC - 1)
                    t_sim.mark(last, str(v))

                def dots(t, v):
                    if v:
                        d_mask.wait(pe, t, "0")
                    elif (t - 1).exists():
                        d_mask.wait(pe, t - 1, "1")
                    for e in range(2):
                        for c in range(DC):
                            last = matmul_split(pe, p_dot[:, e * 512:(e + 1) * 512],
                                                [x[:, c, v * P:(v + 1) * P] for x in hT[t.step % 2]],
                                                [x[:, c, e * 512:(e + 1) * 512] for x in wdown],
                                                c == 0, c == DC - 1)
                    t_dot.mark(last, str(v))

                def hidden(t, k):
                    if k == 0 and (t - 1).exists():
                        d_out.wait(pe, t - 1, "1")
                    if k >= 2:
                        a_hid.wait(pe, t, str(k - 2))
                    elif (t - 1).exists():
                        a_hid.wait(pe, t - 1, str(k + 2))
                    if k == 1:
                        d_hT.wait(pe, t + 1 if (t + 1).exists(last=count) else t)
                    for j in range(2):
                        i = 2 * k + j
                        for c in range(DC):
                            last = matmul_split(pe, p_hid[k % 2][:, j * V * P:(j + 1) * V * P],
                                                [x[:, c, i * P:(i + 1) * P] for x in wup],
                                                [x[:, c, :] for x in hT[t.step % 2]], c == 0, c == DC - 1)
                    t_hid.mark(last, str(k))

                def turn_w(t, v):
                    a_silu.wait(pe, t, str(v))
                    d_clamp.wait(pe, t, f"add{v}")
                    if v:
                        a_wT.wait(pe, t, "0")
                    elif (t - 1).exists():
                        a_wT.wait(pe, t - 1, "1")
                    for e in range(EC):
                        for hd in range(HEADS):
                            last = pe.matmul(p_wT[:, e, :], q[v][:, hd, e * P:(e + 1) * P], ident[:],
                                             is_transpose=True, start=hd == 0, stop=hd == HEADS - 1)
                    t_wT.mark(last, str(v))

                def dense(t, v):
                    if v == 0:
                        a_hid.wait(pe, t, "3")
                    if (t - 1).exists():
                        d_out.wait(pe, t - 1, str(v))
                    for e in range(EC):
                        pe.matmul(p_y[v], hs[:, e, v * P:(v + 1) * P], wdn[:, e, :], start=e == 0, stop=False)

                def experts(t, v):
                    a_wT.wait(pe, t, str(v))
                    for e in range(EC):
                        last = pe.matmul(p_y[v], wT[v][:, e, :], eup[:, e, :], start=False, stop=e == EC - 1)
                    t_out.mark(last, str(v))

                first = Turn(0, 0, unroll)
                turn_h(first)
                similar(first, 0)
                similar(first, 1)
                dots(first, 0)

                def step(t):
                    before, after = (t - 1).exists(), (t + 1).exists(last=count)
                    if before:
                        dense(t - 1, 0)
                    if after:
                        turn_h(t + 1)
                    dots(t, 1)
                    if before:
                        experts(t - 1, 0)
                        dense(t - 1, 1)
                    if after:
                        similar(t + 1, 0)
                    if before:
                        experts(t - 1, 1)
                    if after:
                        similar(t + 1, 1)
                    for k in range(4):
                        hidden(t, k)
                    if after:
                        dots(t + 1, 0)
                    turn_w(t, 0)
                    turn_w(t, 1)
                turns(pe, count, unroll, step)
                end = Turn(0, count - 1, unroll)
                for v in range(V):
                    dense(end, v)
                    experts(end, v)

            @block.scalar
            def _(act):
                def turn_h(t):
                    t_hT.wait(act, t)
                    if (t - 2).exists():
                        t_hid.wait(act, t - 2, "3")
                    a_hT.mark(act.copy(hT[t.step % 2][0][:].rearrange("p c n -> p (c n)"), p_tr[:]))

                def similar(t, v):
                    t_sim.wait(act, t, str(v))
                    if (t - 1).exists():
                        g_grid.wait(act, t - 1, str(v))
                        d_top.wait(act, t - 1, "tm")
                    a_sim.mark(act.copy(sim[:, v, :], p_sim[:]), str(v))

                def exps(t, v):
                    d_mask.wait(act, t, str(v))
                    if v == 0:
                        d_top.wait(act, t, "tm")
                        if (t - 1).exists():
                            d_z.wait(act, t - 1, "z")
                        a_te.mark(act.activation(te[:], tm[:], ACT.Exp))
                    for hd in range(HEADS):
                        last = act.activation(grid[v][:, hd, :], grid[v][:, hd, :], ACT.Exp,
                                              bias=negm[:, v, hd:hd + 1])
                    a_exp.mark(last, str(v))

                def turned(t, v):
                    t_wT.wait(act, t, str(v))
                    if (t - 1).exists():
                        t_out.wait(act, t - 1, str(v))
                    a_wT.mark(act.copy(wT[v][:], p_wT[:]), str(v))

                def hidden(t, k):
                    t_hid.wait(act, t, str(k))
                    if k == 0 and (t - 1).exists():
                        t_out.wait(act, t - 1, "1")
                    a_hid.mark(act.activation(hs[:, 2 * k:2 * k + 2, :],
                                              p_hid[k % 2][:].rearrange("p (j n) -> p j n", j=2), ACT.Silu), str(k))

                def weights(t, v):
                    d_mul.wait(act, t, str(v))
                    a_silu.mark(act.activation(q[v][:], q[v][:], ACT.Silu), str(v))

                first = Turn(0, 0, unroll)
                turn_h(first)
                similar(first, 0)
                similar(first, 1)

                def step(t):
                    after = (t + 1).exists(last=count)
                    if after:
                        turn_h(t + 1)
                    exps(t, 0)
                    exps(t, 1)
                    if after:
                        similar(t + 1, 0)
                        similar(t + 1, 1)
                    hidden(t, 0)
                    hidden(t, 1)
                    weights(t, 0)
                    hidden(t, 2)
                    hidden(t, 3)
                    weights(t, 1)
                    turned(t, 0)
                    turned(t, 1)
                turns(act, count, unroll, step)

            @block.vector
            def _(dve):
                def front(t):
                    slot_wait(dve, s_ld, t)
                    norm.statistics(dve, t)

                def normed(t):
                    if (t - 1).exists():
                        t_hT.wait(dve, t - 1)
                    norm.scale(dve, t, h)

                def turned(t):
                    a_hT.wait(dve, t)
                    x = hT[t.step % 2]
                    d_hT.mark(dve.tensor_tensor(x[1][:].rearrange("p c n -> p (c n)"), p_tr[:],
                                                x[0][:].rearrange("p c n -> p (c n)").bitcast(F32),
                                                ALU.subtract))

                def sides(t, v):
                    a_sim.wait(dve, t, str(v), alone=True)
                    for hd in range(HEADS):
                        sx = sim[:, v, hd * KEYS:(hd + 1) * KEYS]
                        sy = sim[:, v, (HEADS + hd) * KEYS:(HEADS + hd + 1) * KEYS]
                        dve.max(tx[:, v, hd, :], sx)
                        dve.max(ty[:, v, hd, :], sy)
                        last = dve.max(tc[:, v, hd, :], sx[:, XROWS:])
                    if v == V - 1:
                        d_top.mark(last, "maxes")

                def rank(t):
                    d_top.wait(dve, t, "maxes")
                    if (t - 1).exists():
                        a_exp.wait(dve, t - 1, "1")
                    for v in range(V):
                        pairs = lambda a: a[:, v].unsqueeze(3).to_broadcast([P, HEADS, TOP, TOP])
                        across = ty[:, v].unsqueeze(2).to_broadcast([P, HEADS, TOP, TOP])
                        last = dve.tensor_tensor(cand[:, v].rearrange("p h (a b) -> p h a b", a=TOP),
                                                 pairs(tx), across, ALU.add)
                    d_top.mark(last, "cand")
                    for v in range(V):
                        if (t - 1).exists():
                            d_mul.wait(dve, t - 1, str(v))
                        last = dve.tensor_tensor(
                            grid[v][:, :, EXPERTS:].rearrange("p h (a b) -> p h a b", a=TOP),
                            tc[:, v].unsqueeze(3).to_broadcast([P, HEADS, TOP, TOP]),
                            ty[:, v].unsqueeze(2).to_broadcast([P, HEADS, TOP, TOP]), ALU.add)
                    d_top.mark(last, "clamped pairs")
                    d_top.wait(dve, t, "cand", alone=True)
                    for v in range(V):
                        for hd in range(HEADS):
                            last = dve.max(tp[:, v, hd, :], cand[:, v, hd, :])
                    d_top.mark(last, "best")
                    d_top.wait(dve, t, "best")
                    d_top.mark(dve.tensor_scalar(negm[:], tp[:, :, :, 0], -1.0, None, ALU.mult), "negm")
                    d_top.mark(dve.tensor_tensor(tm[:], tp[:], tp[:, :, :, 0:1].to_broadcast([P, V, HEADS, TOP]),
                                                 ALU.subtract), "tm")

                def mask(t, v):
                    t_dot.wait(dve, t, str(v))
                    g_grid.wait(dve, t, str(v))
                    if v == 0:
                        d_top.wait(dve, t, "tm")
                    if (t - 1).exists():
                        t_wT.wait(dve, t - 1, str(v))
                        d_clamp.wait(dve, t - 1, f"add{v}")
                    d_last.mark(dve.tensor_copy(p_last[:, v:v + 1], p_dot[:, EXPERTS - 1:EXPERTS]), str(v))
                    for hd in range(HEADS):
                        dve.scalar_tensor_tensor(out=q[v][:, hd, 0:EXPERTS], in0=grid[v][:, hd, 0:EXPERTS],
                                                 scalar=tp[:, v, hd, TOP - 1:TOP], in1=p_dot[:],
                                                 op0=ALU.is_ge, op1=ALU.mult)
                    d_last.wait(dve, t, str(v))
                    for hd in range(HEADS):
                        last = dve.tensor_scalar(q[v][:, hd, EXPERTS:], grid[v][:, hd, EXPERTS:],
                                                 tp[:, v, hd, TOP - 1:TOP], p_last[:, v:v + 1],
                                                 ALU.is_ge, ALU.mult)
                    d_mask.mark(last, str(v))

                def sums(t):
                    a_te.wait(dve, t)
                    d_z.mark(dve.tensor_reduce(z[:], te[:], AX.X, ALU.add), "z")
                    d_z.wait(dve, t, "z")
                    d_z.mark(dve.reciprocal(rz[:], z[:]), "rz")
                    d_z.wait(dve, t, "rz")

                def weigh(t, v):
                    d_mask.wait(dve, t, str(v))
                    a_exp.wait(dve, t, str(v))
                    for hd in range(HEADS):
                        last = dve.scalar_tensor_tensor(out=q[v][:, hd, :], in0=q[v][:, hd, :],
                                                        scalar=rz[:, v, hd:hd + 1], in1=grid[v][:, hd, :],
                                                        op0=ALU.mult, op1=ALU.mult)
                    d_mul.mark(last, str(v))

                def clamp(t, v):
                    a_silu.wait(dve, t, str(v))
                    d_clamp.mark(dve.tensor_reduce(clamped[:, v:v + 1], q[v][:, :, EXPERTS:], AX.XY, ALU.add), f"sum{v}")
                    d_clamp.wait(dve, t, f"sum{v}")
                    d_clamp.mark(dve.tensor_tensor(q[v][:, 0, EXPERTS - 1:EXPERTS], q[v][:, 0, EXPERTS - 1:EXPERTS],
                                                   clamped[:, v:v + 1], ALU.add), f"add{v}")

                def output(t, v):
                    t_out.wait(dve, t, str(v))
                    if v == 0 and (t - 2).exists():
                        slot_wait(dve, s_st, t - 2)
                    d_out.mark(dve.scalar_tensor_tensor(
                        out=yt[t.step % 2][:, v, :], in0=p_y[v], scalar=0.5,
                        in1=xt[t.step % 4][:, v, :], op0=ALU.mult, op1=ALU.add), str(v))

                first = Turn(0, 0, unroll)
                front(first)
                normed(first)
                turned(first)
                front(first + 1)
                sides(first, 0)
                sides(first, 1)
                rank(first)
                normed(first + 1)

                def step(t):
                    before, after = (t - 1).exists(), (t + 1).exists(last=count)
                    mask(t, 0)
                    if (t + 2).exists(last=count):
                        front(t + 2)
                    if after:
                        turned(t + 1)
                    sums(t)
                    mask(t, 1)
                    weigh(t, 0)
                    if before:
                        output(t - 1, 0)
                        output(t - 1, 1)
                    weigh(t, 1)
                    if (t + 2).exists(last=count):
                        normed(t + 2)
                    if after:
                        sides(t + 1, 0)
                    clamp(t, 0)
                    if after:
                        sides(t + 1, 1)
                        rank(t + 1)
                    clamp(t, 1)
                turns(dve, count, unroll, step)
                end = Turn(0, count - 1, unroll)
                output(end, 0)
                output(end, 1)


def channel_mix(nc, name, src, dst, w):
    with ExitStack() as ctx:
        m = Memory(nc, ctx, name)
        T = S // P
        wr, wk, wv = (m.sbuf(k, DC, D) for k in ("wr", "wk", "wv"))
        mu = m.sbuf("mu", 2, DC)
        ident, half = m.sbuf("ident", P), m.sbuf("half", 1)
        xt = [m.sbuf(f"xt{k}", T, D) for k in range(4)]
        yt = [m.sbuf(f"yt{k}", T, D) for k in range(2)]
        h = m.sbuf("h", T, D)
        hT = m.sbuf("hT", DC, 1 + S)
        diff = m.sbuf("diff", DC, S)
        xr, xk = ([m.sbuf(f"{n}{k}", DC, S) for k in range(2)] for n in ("xr", "xk"))
        rs, ks, rk = m.sbuf("rs", T, D), m.sbuf("ks", DC, S), m.sbuf("rk", T, D)
        p_tr, p_k = m.psum("p_tr", DC, S), m.psum("p_k", DC, S)
        p_r, p_v = m.psum("p_r", T, D), m.psum("p_v", T, D)

        s_w, s_id, s_z = m.sem("s_w"), m.sem("s_id"), m.sem("s_z")
        s_ld = [m.track(f"s_ld{k}", inc=16) for k in range(4)]
        s_st = [m.track(f"s_st{k}", inc=16) for k in range(2)]
        norm = Norm(m, T, lambda t: xt[t.step % 4], half)
        t_hT, a_hT = m.track("t_hT"), m.track("a_hT")
        d_mix = m.track("d_mix", "diff", "xk", "xr")
        t_k, t_r, t_v = m.track("t_k"), m.track("t_r"), m.track("t_v")
        a_k = m.track("a_k", "relu", "square")
        a_r = m.track("a_r")
        d_out = m.track("d_out", "rk", "y")
        count, unroll = B, 4

        with nc.Block() as block:
            @block.sync
            def _(sp):
                def load(t):
                    sp.dma_start(xt[t.step % 4][:], row_tiles(src, t)).then_inc(s_ld[t.step % 4].sem, 16)

                load(Turn(0, 0, unroll))
                sp.dma_start(ident[:], w["ident"]).then_inc(s_id, 16)
                for t, k in ((wr, "wr"), (wk, "wk"), (wv, "wv")):
                    sp.dma_start(t[:], w[k].rearrange("(c p) d -> p c d", p=P)).then_inc(s_w, 16)
                with nc.allow_non_contiguous_dma(reason="256 words, once"):
                    for n, k in enumerate(("mu_r", "mu_k")):
                        sp.dma_start(mu[:, n, :], w[k].rearrange("(c p) -> p c", p=P)).then_inc(s_w, 16)

                def store(t):
                    d_out.wait(sp, t, "y")
                    sp.dma_start(row_tiles(dst, t), yt[t.step % 2][:]).then_inc(s_st[t.step % 2].sem, 16)

                for n in range(1, 3):
                    load(Turn(0, n, unroll))

                def step(t):
                    if (t - 1).exists():
                        store(t - 1)
                    if (t + 3).exists(last=count):
                        load(t + 3)
                turns(sp, count, unroll, step)
                store(Turn(0, count - 1, unroll))
                for k in range(2):
                    sp.wait_ge(s_st[k].sem, 16 * (count // 2))

            @block.gpsimd
            def _(pool):
                pool.wait_ge(s_z, 2)
                norm.root(pool, Turn(0, 0, unroll))
                norm.root(pool, Turn(0, 1, unroll))

                def step(t):
                    if (t + 2).exists(last=count):
                        norm.root(pool, t + 2)
                turns(pool, count, unroll, step)

            @block.tensor
            def _(pe):
                pe.wait_ge(s_id, 16)

                def turn_h(t):
                    norm.d_h.wait(pe, t)
                    if (t - 1).exists():
                        a_hT.wait(pe, t - 1)
                    for v in range(T):
                        for c in range(DC):
                            last = pe.transpose(p_tr[:, c, v * P:(v + 1) * P], h[:, v, c * P:(c + 1) * P], ident[:])
                    t_hT.mark(last)

                def keys(t):
                    d_mix.wait(pe, t, "xk")
                    if (t - 1).exists():
                        a_k.wait(pe, t - 1, "relu")
                    for i in range(DC):
                        for c in range(DC):
                            last = pe.matmul(p_k[:, i, :], wk[:, c, i * P:(i + 1) * P], xk[t.step % 2][:, c, :],
                                             start=c == 0, stop=c == DC - 1)
                    t_k.mark(last)

                def receptance(t):
                    d_mix.wait(pe, t, "xr")
                    if (t - 1).exists():
                        a_r.wait(pe, t - 1)
                    for v in range(T):
                        for c in range(DC):
                            last = pe.matmul(p_r[:, v, :], xr[t.step % 2][:, c, v * P:(v + 1) * P], wr[:, c, :],
                                             start=c == 0, stop=c == DC - 1)
                    t_r.mark(last)

                def values(t):
                    a_k.wait(pe, t, "square")
                    if (t - 1).exists():
                        d_out.wait(pe, t - 1, "rk")
                    for v in range(T):
                        for c in range(DC):
                            last = pe.matmul(p_v[:, v, :], ks[:, c, v * P:(v + 1) * P], wv[:, c, :],
                                             start=c == 0, stop=c == DC - 1)
                    t_v.mark(last)

                turn_h(Turn(0, 0, unroll))
                pe.wait_ge(s_w, 16 * 5)

                def step(t):
                    if (t + 1).exists(last=count):
                        turn_h(t + 1)
                    keys(t)
                    receptance(t)
                    values(t)
                turns(pe, count, unroll, step)

            @block.scalar
            def _(act):
                act.wait_ge(s_z, 1)

                def turned(t):
                    t_hT.wait(act, t)
                    if (t - 1).exists():
                        d_mix.wait(act, t - 1, "xr")
                    a_hT.mark(act.copy(hT[:, :, 1:], p_tr[:]))

                turned(Turn(0, 0, unroll))

                def step(t):
                    if (t + 1).exists(last=count):
                        turned(t + 1)
                    t_k.wait(act, t)
                    if (t - 1).exists():
                        t_v.wait(act, t - 1)
                    a_k.mark(act.activation(ks[:], p_k[:], ACT.Relu), "relu")
                    a_k.wait(act, t, "relu")
                    a_k.mark(act.activation(ks[:], ks[:], ACT.Square), "square")
                    t_r.wait(act, t)
                    if (t - 1).exists():
                        d_out.wait(act, t - 1, "rk")
                    a_r.mark(act.activation(rs[:], p_r[:], ACT.Sigmoid))
                turns(act, count, unroll, step)

            @block.vector
            def _(dve):
                dve.memset(hT[:, :, 0:1], 0.0).then_inc(s_z, 1)
                dve.memset(half[:], -0.5).then_inc(s_z, 1)

                def mix(t):
                    a_hT.wait(dve, t)
                    d_mix.mark(dve.tensor_tensor(diff[:], hT[:, :, 1:], hT[:, :, 0:S], ALU.subtract), "diff")
                    d_mix.wait(dve, t, "diff")
                    for n, out, free, mark in ((1, xk, t_k, "xk"), (0, xr, t_r, "xr")):
                        if (t - 2).exists():
                            free.wait(dve, t - 2)
                        for c in range(DC):
                            last = dve.scalar_tensor_tensor(out=out[t.step % 2][:, c, :], in0=diff[:, c, :], scalar=mu[:, n, c:c + 1],
                                                            in1=hT[:, c, 0:S], op0=ALU.mult, op1=ALU.add)
                        d_mix.mark(last, mark)

                def output(t):
                    t_v.wait(dve, t)
                    a_r.wait(dve, t)
                    if (t - 1).exists():
                        d_out.wait(dve, t - 1, "y")
                    d_out.mark(dve.tensor_tensor(rk[:], p_v[:], rs[:], ALU.mult), "rk")
                    d_out.wait(dve, t, "rk")
                    if (t - 2).exists():
                        slot_wait(dve, s_st, t - 2)
                    d_out.mark(dve.scalar_tensor_tensor(
                        out=yt[t.step % 2][:], in0=rk[:], scalar=0.5, in1=xt[t.step % 4][:],
                        op0=ALU.mult, op1=ALU.add), "y")

                def front(t):
                    slot_wait(dve, s_ld, t)
                    norm.statistics(dve, t)
                    if (t - 1).exists():
                        t_hT.wait(dve, t - 1)
                    norm.scale(dve, t, h)

                front(Turn(0, 0, unroll))
                dve.wait_ge(s_w, 16 * 5)
                mix(Turn(0, 0, unroll))
                front(Turn(0, 1, unroll))

                def step(t):
                    if (t + 1).exists(last=count):
                        mix(t + 1)
                    if (t + 2).exists(last=count):
                        front(t + 2)
                    output(t)
                turns(dve, count, unroll, step)


MH, HD = 16, D // 16
SLOT = 32
BR = 2
SEGS = S // P
BRANCH_WEIGHT = float(np.float32(1) / np.float32(3))


def dilated_attention(nc, name, src, dst, w):
    with ExitStack() as ctx:
        m = Memory(nc, ctx, name)
        UR = BR * SEGS
        PADW = MH * SLOT
        wq, wk = ([[m.sbuf(f"w{n}{br}{k}", DC, PADW, dt=F32R) for k in "hl"] for br in range(BR)] for n in "qk")
        wv = [[m.sbuf(f"wv{br}{k}", DC, D, dt=F32R) for k in "hl"] for br in range(BR)]
        wo = m.sbuf("wo", BR, DC, D)
        ones = m.sbuf("ones", 2, SLOT)
        bq, bk = m.sbuf("bq", BR, 4), m.sbuf("bk", BR, 4)
        bqs, bk1 = m.sbuf("bqs", BR, 4), m.sbuf("bk1", BR, 4)
        slots = m.sbuf("slots", 4)
        kone = m.sbuf("kone", 1)
        bv, bo, bos = m.sbuf("bv", BR, D), m.sbuf("bo", BR, D), m.sbuf("bos", 2, D)
        ident, half = m.sbuf("ident", P), m.sbuf("half", 1)
        with ExitStack() as sub:
            load_split(nc, Memory(nc, sub, name + "w"),
                       [(w[n][br, c * P:(c + 1) * P, :], t[br][0][:, c, :], t[br][1][:, c, :], heads)
                        for n, t, heads in (("aq", wq, (HD, SLOT)), ("ak", wk, (HD, SLOT)), ("av", wv, None))
                        for br in range(BR) for c in range(DC)])

        xt = [m.sbuf(f"xt{k}", SEGS, D) for k in range(2)]
        xb = [m.sbuf(f"xb{k}", SEGS, D) for k in range(2)]
        yt = [m.sbuf(f"yt{k}", SEGS, D) for k in range(2)]
        h = m.sbuf("h", SEGS, D)
        hT = [[m.sbuf(f"hT{r}{k}", DC, S, dt=F32R) for k in "hl"] for r in range(2)]
        qT = [m.sbuf(f"qT{br}", 4, S) for br in range(BR)]
        kT = [m.sbuf(f"kT{br}", 4, S) for br in range(BR)]
        va = [m.sbuf(f"va{br}", SEGS, MH // 2, 4, HD) for br in range(BR)]
        kz = [m.sbuf(f"kz{k}", 4, 4, P) for k in range(2)]
        mpad = m.sbuf("mpad", 4, P)
        qa = m.sbuf("qa", 4, P)
        ex = m.sbuf("ex", 4, 4, P)
        rden = m.sbuf("rden", DC, P)
        oT = [[m.sbuf(f"oT{r}{br}", DC, S) for br in range(BR)] for r in range(2)]

        p_s = [m.psum(f"p_s{c}", 4, P) for c in range(4)]
        p_m, p_pr, p_x = (m.psum(k, 512) for k in ("p_m", "p_pr", "p_x"))
        p_av = m.psum("p_av", 2, DC, P)

        s_w, s_id, s_z, s_c = m.sem("s_w"), m.sem("s_id"), m.sem("s_z"), m.sem("s_c")
        rows, units = B, B * UR
        WEIGHT_DMAS = 5 + 4 * 2
        s_ld = [m.track(f"s_ld{k}", inc=16) for k in range(2)]
        s_st = [m.track(f"s_st{k}", inc=16) for k in range(2)]
        norm = Norm(m, SEGS, lambda r: xt[r.step % 2], half)
        g_xb = m.track("g_xb")
        t_hT, a_hT, d_hT = (m.track(k, "0", "1") for k in ("t_hT", "a_hT", "d_hT"))
        t_q, t_k, t_v, a_q, a_k, d_v = (m.track(k) for k in ("t_q", "t_k", "t_v", "a_q", "a_k", "d_v"))
        banks = [str(b) for b in range(4)]
        t_s, d_max, t_st, a_ex = (m.track(k, *banks) for k in ("t_s", "d_max", "t_st", "a_ex"))
        g_kz = m.track("g_kz")
        t_m, d_qa, t_av = m.track("t_m"), m.track("d_qa"), m.track("t_av")
        d_o = m.track("d_o", "rden", "o")
        t_y, d_y = m.track("t_y", *banks), m.track("d_y", *banks)

        row_of = lambda t: Turn(t.group, t.step // UR, 2)
        ur_of = lambda t: t.step % UR
        first_unit, first_row = Turn(0, 0, 2 * UR), Turn(0, 0, 2)
        OUT_AT = 2

        def tokens(a, br, n, count):
            if br == 0:
                return a[:, n:n + count]
            return a.rearrange("p (k two) -> p two k", two=2)[:, n // (S // 2):(n + count - 1) // (S // 2) + 1,
                                                              n % (S // 2):(n % (S // 2)) + min(count, S // 2)]

        with nc.Block() as block:
            @block.sync
            def _(sp):
                def load(r):
                    sp.dma_start(xt[r.step % 2][:], row_tiles(src, r)).then_inc(s_ld[r.step % 2].sem, 16)

                load(first_row)
                sp.dma_start(ident[:], w["ident"]).then_inc(s_id, 16)
                sp.wait_ge(s_z, 2)
                for b in range(4):
                    for t, k in ((bq, "abq"), (bk, "abk")):
                        sp.dma_start(t[SLOT * b:SLOT * b + HD, :, :], w[k][:, b].rearrange("r d c -> d r c")).then_inc(s_w, 16)
                sp.dma_start(kone[:], w["kone"]).then_inc(s_w, 16)
                sp.dma_start(slots[:], w["slots"]).then_inc(s_w, 16)
                for t, k in ((bv, "abv"), (bo, "abo")):
                    sp.dma_start(t[:].rearrange("p r d -> p (r d)"),
                                 w[k].rearrange("(o r) d -> o (r d)", o=1).to_broadcast([P, BR * D])).then_inc(s_w, 16)
                sp.dma_start(wo[:], w["ao"].rearrange("r (c p) d -> p r c d", p=P)).then_inc(s_w, 16)
                load(first_row + 1)

                def store(r):
                    d_y.wait(sp, r)
                    sp.dma_start(row_tiles(dst, r), yt[r.step % 2][:]).then_inc(s_st[r.step % 2].sem, 16)

                def step(r):
                    if (r + 2).exists(last=rows):
                        norm.d_h.wait(sp, r)
                        g_xb.wait(sp, r)
                        load(r + 2)
                    if (r - 1).exists():
                        store(r - 1)
                turns(sp, rows, 2, step)
                store(Turn(0, rows - 1, 2))
                for k in range(2):
                    sp.wait_ge(s_st[k].sem, 16 * (rows // 2))

            @block.gpsimd
            def _(pool):
                pool.wait_ge(s_c, 1)

                def biased(r):
                    slot_wait(pool, s_ld, r)
                    if (r - 2).exists():
                        d_y.wait(pool, r - 2)
                    for v in range(SEGS):
                        last = pool.tensor_tensor(xb[r.step % 2][:, v, :], xt[r.step % 2][:, v, :], bos[:, 1, :], ALU.add)
                    g_xb.mark(last)

                norm.root(pool, first_row)
                pool.wait_ge(s_w, 16 * WEIGHT_DMAS)
                pool.wait_ge(s_c, 6)
                norm.root(pool, first_row + 1)
                biased(first_row)

                def spread(t):
                    br, j = ur_of(t) // SEGS, t.step % SEGS
                    if j == 0:
                        a_k.wait(pool, t + (SEGS - 1))
                    if (t - 2).exists():
                        t_st.wait(pool, t - 2)
                    for b in range(4):
                        last = pool.tensor_tensor(kz[t.step % 2][:, :, b, :], kT[br][:, :, j * P:(j + 1) * P],
                                                  slots[:, b:b + 1].unsqueeze(2).to_broadcast([P, 4, P]), ALU.mult)
                    g_kz.mark(last)

                spread(first_unit)

                def step(t):
                    if (t + 1).exists(last=units):
                        spread(t + 1)
                    u, r = ur_of(t), row_of(t)
                    if u == 5 and (r + 2).exists(last=rows):
                        norm.root(pool, r + 2)
                    if u == 7 and (r + 1).exists(last=rows):
                        biased(r + 1)
                turns(pool, units, 2 * UR, step)

            @block.tensor
            def _(pe):
                pe.wait_ge(s_id, 16)

                def turn_h(r, j):
                    norm.d_h.wait(pe, r)
                    for v in range(2):
                        for c in range(DC):
                            last = pe.transpose(p_x[:, (c * 2 + v) * P:(c * 2 + v + 1) * P],
                                                h[:, 2 * j + v, c * P:(c + 1) * P], ident[:])
                    t_hT.mark(last, str(j))

                def target(t):
                    u = ur_of(t)
                    return hT[(t.step // UR) % 2], u // SEGS, u % SEGS

                def projected(pe, t):
                    if (t - 1).exists():
                        d_v.wait(pe, t - 1)

                def query(t):
                    x, br, j = target(t)
                    if br == 0 and j == 0:
                        r = row_of(t)
                        a_hT.wait(pe, r, "1")
                        d_hT.wait(pe, r, "1")
                    projected(pe, t)
                    for c in range(DC):
                        last = matmul_split(pe, p_pr[:], [a[:, c, j * P:(j + 1) * P] for a in wq[br]],
                                            [tokens(a[:, c, :], br, 0, S) for a in x], c == 0, c == DC - 1)
                    t_q.mark(last)

                def key(t):
                    x, br, j = target(t)
                    a_q.wait(pe, t)
                    for c in range(DC):
                        last = matmul_split(pe, p_pr[:], [a[:, c, j * P:(j + 1) * P] for a in wk[br]],
                                            [tokens(a[:, c, :], br, 0, S) for a in x], c == 0, c == DC - 1)
                    t_k.mark(last)

                def value(t):
                    x, br, j = target(t)
                    a_k.wait(pe, t)
                    for c in range(DC):
                        last = matmul_split(pe, p_pr[:, 0:D], [tokens(a[:, c, :], br, j * P, P) for a in x],
                                            [a[:, c, :] for a in wv[br]], c == 0, c == DC - 1)
                    t_v.mark(last)

                def scores(t):
                    br, j = ur_of(t) // SEGS, t.step % SEGS
                    if j == 0:
                        a_q.wait(pe, t + (SEGS - 1))
                    g_kz.wait(pe, t)
                    for c in range(4):
                        if (t - 1).exists():
                            a_ex.wait(pe, t - 1, str(c))
                        t_s.mark(pe.matmul(p_s[c][:].rearrange("p b n -> p (b n)"), qT[br][:, c, j * P:(j + 1) * P],
                                           kz[t.step % 2][:, c].rearrange("p b n -> p (b n)"),
                                           start=True, stop=True), str(c))

                def maxima(t):
                    d_max.wait(pe, t, "3")
                    if (t - 1).exists():
                        d_qa.wait(pe, t - 1)
                    for c in range(4):
                        last = pe.transpose(p_m[:, c * P:(c + 1) * P], mpad[:, c, :], ident[:])
                    t_m.mark(last)

                def scores_t(t):
                    d_qa.wait(pe, t)
                    for c in range(4):
                        for b in range(4):
                            last = pe.matmul(p_s[c][:, b, :], kz[t.step % 2][:, c, b, :], qa[:, c, :],
                                             start=True, stop=True)
                        t_st.mark(last, str(c))

                def attend(t):
                    br, j = ur_of(t) // SEGS, t.step % SEGS
                    a_ex.wait(pe, t, "3")
                    d_v.wait(pe, t)
                    if (t - 1).exists():
                        d_o.wait(pe, t - 1)
                    for c in range(DC):
                        for kind in range(2):
                            for odd in range(2):
                                for b in range(4):
                                    hd = 8 * c + 2 * b + odd
                                    lhs = (va[br][:, j, hd // 2, 2 * odd:2 * odd + 2, :].rearrange("p a d -> p (a d)"),
                                           ones[:, odd, :])[kind]
                                    last = pe.matmul(p_av[SLOT * b:SLOT * (b + 1), kind, c, :], lhs,
                                                     ex[:, hd // 4, hd % 4, :], start=odd == 0, stop=odd == 1)
                    t_av.mark(last)

                def x_free(t):
                    if (t - 1).exists():
                        u, r = ur_of(t - 1), row_of(t - 1)
                        if u < 2 and (r + 1).exists(last=rows):
                            d_hT.wait(pe, r + 1, str(u))
                        if OUT_AT <= u < OUT_AT + 4 and (r - 1).exists():
                            d_y.wait(pe, r - 1, str(u - OUT_AT))

                def put_out(r, v):
                    if v == 0:
                        d_o.wait(pe, Turn(r.group, r.step * UR + UR - 1, 2 * UR))
                    for br in range(BR):
                        for c in range(DC):
                            last = pe.matmul(p_x[:, 0:D], oT[r.step % 2][br][:, c, v * P:(v + 1) * P], wo[:, br, c, :],
                                             start=br == c == 0, stop=(br, c) == (BR - 1, DC - 1))
                    t_y.mark(last, str(v))

                for j in range(2):
                    if j:
                        d_hT.wait(pe, first_row, "0")
                    turn_h(first_row, j)
                d_hT.wait(pe, first_row, "1")
                for j in range(SEGS):
                    query(first_unit + j)
                    key(first_unit + j)
                    value(first_unit + j)
                pe.wait_ge(s_w, 16 * WEIGHT_DMAS)
                pe.wait_ge(s_c, 6)

                def step(t):
                    u, r = ur_of(t), row_of(t)
                    ahead = (t + SEGS).exists(last=units)
                    x_free(t)
                    if u < 2 and (r + 1).exists(last=rows):
                        turn_h(r + 1, u)
                    if OUT_AT <= u < OUT_AT + 4 and (r - 1).exists():
                        put_out(r - 1, u - OUT_AT)
                    if ahead:
                        query(t + SEGS)
                    scores(t)
                    if ahead:
                        key(t + SEGS)
                    maxima(t)
                    if (t - 1).exists():
                        attend(t - 1)
                    if ahead:
                        value(t + SEGS)
                    scores_t(t)
                turns(pe, units, 2 * UR, step)
                end = first_unit + (units - 1)
                end = Turn(end.group, end.step, 2 * UR)
                attend(end)
                for v in range(4):
                    if v:
                        d_y.wait(pe, first_row + (rows - 1), str(v - 1))
                    put_out(first_row + (rows - 1), v)

            @block.scalar
            def _(act):
                def turn_h(r, j):
                    t_hT.wait(act, r, str(j))
                    a_hT.mark(act.copy(hT[r.step % 2][0][:, :, j * 2 * P:(j + 1) * 2 * P],
                                       p_x[:].rearrange("p (c n) -> p c n", c=DC)), str(j))

                def query(t):
                    br, j = ur_of(t) // SEGS, t.step % SEGS
                    t_q.wait(act, t)
                    a_q.mark(act.activation(qT[br][:, j, :], p_pr[:], ACT.Identity, bias=bqs[:, br, j:j + 1], scale=HD ** -0.5))

                def key(t):
                    br, j = ur_of(t) // SEGS, t.step % SEGS
                    t_k.wait(act, t)
                    a_k.mark(act.activation(kT[br][:, j, :], p_pr[:], ACT.Identity, bias=bk1[:, br, j:j + 1]))

                def exps(t):
                    if (t - 1).exists():
                        t_av.wait(act, t - 1)
                    for c in range(4):
                        t_st.wait(act, t, str(c))
                        a_ex.mark(act.activation(ex[:, c, :, :], p_s[c][:], ACT.Exp), str(c))

                for j in range(2):
                    turn_h(first_row, j)
                act.wait_ge(s_c, 6)
                for j in range(SEGS):
                    query(first_unit + j)
                    key(first_unit + j)

                def step(t):
                    u, r = ur_of(t), row_of(t)
                    if u < 2 and (r + 1).exists(last=rows):
                        turn_h(r + 1, u)
                    ahead = (t + SEGS).exists(last=units)
                    if ahead:
                        query(t + SEGS)
                    if ahead:
                        key(t + SEGS)
                    exps(t)
                turns(act, units, 2 * UR, step)

            @block.vector
            def _(dve):
                dve.memset(bq[:], 0.0).then_inc(s_z, 1)
                dve.memset(bk[:], 0.0).then_inc(s_z, 1)
                dve.memset(half[:], -0.5).then_inc(s_c, 1)
                dve.memset(mpad[:], 0.0).then_inc(s_c, 1)
                for br in range(BR):
                    dve.memset(va[br][:, :, :, 1:3, :], 0.0)
                for odd in range(2):
                    dve.memset(ones[:, odd, odd * HD:(odd + 1) * HD], 1.0)
                    last = dve.memset(ones[:, odd, (1 - odd) * HD:(2 - odd) * HD], 0.0)
                last.then_inc(s_c, 1)

                def turn_h(r, j):
                    a_hT.wait(dve, r, str(j))
                    x = hT[r.step % 2]
                    cols = slice(j * 2 * P, (j + 1) * 2 * P)
                    d_hT.mark(dve.tensor_tensor(x[1][:, :, cols], p_x[:].rearrange("p (c n) -> p c n", c=DC),
                                                x[0][:, :, cols].bitcast(F32), ALU.subtract), str(j))

                def value(t):
                    br, j = ur_of(t) // SEGS, t.step % SEGS
                    t_v.wait(dve, t)
                    pairs = "p (h two d) -> p h two d"
                    d_v.mark(dve.tensor_tensor(va[br][:, j, :, 0:4:3, :], p_pr[:, 0:D].rearrange(pairs, two=2, d=HD),
                                               bv[:, br, :].rearrange(pairs, two=2, d=HD), ALU.add))

                def maxima(t):
                    if (t - 1).exists():
                        t_m.wait(dve, t - 1)
                    for c in range(4):
                        t_s.wait(dve, t, str(c))
                        d_max.mark(dve.tensor_reduce(mpad[:, c, HD::SLOT], p_s[c][:], AX.X, ALU.max, negate=True), str(c))

                def divide(t):
                    br, j = ur_of(t) // SEGS, t.step % SEGS
                    r = row_of(t)
                    t_av.wait(dve, t)
                    if (t - 1).exists():
                        d_o.wait(dve, t - 1)
                    d_o.mark(dve.reciprocal(rden[:], p_av[:, 1]), "rden")
                    d_o.wait(dve, t, "rden")
                    if ur_of(t) == 0 and (r - 2).exists():
                        t_y.wait(dve, r - 2, "3")
                    to = oT[r.step % 2][br]
                    if br == 0:
                        to = to[:, :, j * P:(j + 1) * P]
                    else:
                        off, s = j // 2, j % 2
                        to = to[:].rearrange("p c (k two) -> p c two k", two=2)[:, :, off, s * P:(s + 1) * P]
                    d_o.mark(dve.tensor_tensor(to, p_av[:, 0], rden[:], ALU.mult), "o")

                def augment(t):
                    br, j = ur_of(t) // SEGS, t.step % SEGS
                    t_m.wait(dve, t)
                    if (t - 1).exists():
                        t_st.wait(dve, t - 1, "3")
                    d_qa.mark(dve.tensor_tensor(qa[:], p_m[:].rearrange("p (c n) -> p c n", c=4),
                                                qT[br][:, :, j * P:(j + 1) * P], ALU.add))

                def put_out(r, v):
                    t_y.wait(dve, r, str(v))
                    if v == 0:
                        g_xb.wait(dve, r)
                        if (r - 2).exists():
                            slot_wait(dve, s_st, r - 2)
                    d_y.mark(dve.scalar_tensor_tensor(out=yt[r.step % 2][:, v, :], in0=p_x[:, 0:D], scalar=BRANCH_WEIGHT,
                                                      in1=xb[r.step % 2][:, v, :], op0=ALU.mult, op1=ALU.add), str(v))

                def statistics(r):
                    slot_wait(dve, s_ld, r)
                    norm.statistics(dve, r)

                def scale(r):
                    if (r - 1).exists():
                        t_hT.wait(dve, r - 1, "1")
                    norm.scale(dve, r, h)

                statistics(first_row)
                scale(first_row)
                for j in range(2):
                    turn_h(first_row, j)
                dve.wait_ge(s_w, 16 * WEIGHT_DMAS)
                dve.tensor_scalar(bqs[:], bq[:], HD ** -0.5, None, ALU.mult)
                dve.tensor_scalar(bk1[:], bk[:], kone[:, 0:1], None, ALU.add).then_inc(s_c, 1)
                dve.tensor_tensor(bos[:, 0, :], bo[:, 0, :], bo[:, 1, :], ALU.add).then_inc(s_c, 1)
                dve.wait_ge(s_c, 5)
                dve.tensor_scalar(bos[:, 1, :], bos[:, 0, :], BRANCH_WEIGHT, None, ALU.mult).then_inc(s_c, 1)
                for j in range(SEGS):
                    value(first_unit + j)
                statistics(first_row + 1)
                scale(first_row + 1)

                def step(t):
                    u, r = ur_of(t), row_of(t)
                    if u < 2 and (r + 1).exists(last=rows):
                        turn_h(r + 1, u)
                    if OUT_AT <= u < OUT_AT + 4 and (r - 1).exists():
                        put_out(r - 1, u - OUT_AT)
                    maxima(t)
                    augment(t)
                    if (t + SEGS).exists(last=units):
                        value(t + SEGS)
                    if (t - 1).exists():
                        divide(t - 1)
                    if (r + 2).exists(last=rows):
                        if u == 4:
                            statistics(r + 2)
                        if u == 6:
                            scale(r + 2)
                turns(dve, units, 2 * UR, step)
                divide(Turn(0, units - 1, 2 * UR))
                for v in range(4):
                    put_out(first_row + (rows - 1), v)


UNSEEN = 1e-9
NB = S // P


def batch_attention(nc, name, src, dst, w):
    scratch = {k: nc.dram_tensor(f"{name}_{k}", (P, B * DC * S), F32, kind="Internal").ap() for k in "qkv"}
    project(nc, name + "p", src, scratch, w)
    attend_batch(nc, name + "s", src, dst, scratch, w)


def project(nc, name, src, scratch, w):
    with ExitStack() as ctx:
        m = Memory(nc, ctx, name)
        wq, wk, wv = ([m.sbuf(f"w{n}{k}", DC, D, dt=F32R) for k in "hl"] for n in "qkv")
        with ExitStack() as sub:
            load_split(nc, Memory(nc, sub, name + "w"),
                       [(w[n][c * P:(c + 1) * P, :], t[0][:, c, :], t[1][:, c, :], None)
                        for n, t in (("bq", wq), ("bk", wk), ("bv", wv)) for c in range(DC)])
        ident, half = m.sbuf("ident", P), m.sbuf("half", 1)
        xt = [m.sbuf(f"xt{k}", NB, D) for k in range(4)]
        h = m.sbuf("h", NB, D)
        hT = [[m.sbuf(f"hT{r}{k}", DC, S, dt=F32R) for k in "hl"] for r in range(2)]
        qT = [m.sbuf(f"qT{k}", DC, S) for k in range(2)]
        kT = [m.sbuf(f"kT{k}", DC, S) for k in range(2)]
        vs = [m.sbuf(f"vs{k}", NB, D) for k in range(2)]
        p_tr, p_q, p_k, p_v = (m.psum(k, DC, S) for k in ("p_tr", "p_q", "p_k", "p_v"))
        s_w, s_c = m.sem("s_w"), m.sem("s_c")
        s_ld = [m.track(f"s_ld{k}", inc=16) for k in range(4)]
        s_q, s_k, s_v = ([m.track(f"s_{n}{k}", inc=16) for k in range(2)] for n in "qkv")
        norm = Norm(m, NB, lambda t: xt[t.step % 4], half)
        t_hT, a_hT, d_hT = m.track("t_hT"), m.track("a_hT"), m.track("d_hT")
        t_q, t_k, t_v = m.track("t_q"), m.track("t_k"), m.track("t_v")
        a_q, a_k, d_v = m.track("a_q"), m.track("a_k"), m.track("d_v")
        count, unroll = B, 4
        first = Turn(0, 0, unroll)

        with nc.Block() as block:
            @block.sync
            def _(sp):
                sp.dma_start(ident[:], w["ident"]).then_inc(s_w, 16)

                def load(t):
                    sp.dma_start(xt[t.step % 4][:], row_tiles(src, t)).then_inc(s_ld[t.step % 4].sem, 16)

                for n in range(3):
                    load(first + n)

                def step(t):
                    if (t + 3).exists(last=count):
                        if (t - 1).exists():
                            norm.d_h.wait(sp, t - 1)
                        load(t + 3)
                    cols = bass.ds(t.times(DC * S, 0), DC * S)
                    for n, written, buf, sems in (("q", a_q, qT, s_q), ("k", a_k, kT, s_k), ("v", d_v, vs, s_v)):
                        written.wait(sp, t)
                        sp.dma_start(scratch[n][:, cols], buf[t.step % 2][:].rearrange("p a b -> p (a b)")
                                     ).then_inc(sems[t.step % 2].sem, 16)
                turns(sp, count, unroll, step)
                for k in range(2):
                    for sems in (s_q, s_k, s_v):
                        sp.wait_ge(sems[k].sem, 16 * (count // 2))

            @block.gpsimd
            def _(pool):
                pool.wait_ge(s_c, 1)
                norm.root(pool, first)

                def step(t):
                    if (t + 1).exists(last=count):
                        norm.root(pool, t + 1)
                turns(pool, count, unroll, step)

            @block.tensor
            def _(pe):
                pe.wait_ge(s_w, 16)

                def turn_h(t):
                    norm.d_h.wait(pe, t)
                    if (t - 1).exists():
                        d_hT.wait(pe, t - 1)
                    for v in range(NB):
                        for c in range(DC):
                            last = pe.transpose(p_tr[:, c, v * P:(v + 1) * P], h[:, v, c * P:(c + 1) * P], ident[:])
                    t_hT.mark(last)

                turn_h(first)

                def step(t):
                    x = hT[t.step % 2]
                    a_hT.wait(pe, t)
                    d_hT.wait(pe, t)
                    if (t - 1).exists():
                        a_q.wait(pe, t - 1)
                    for i in range(DC):
                        for c in range(DC):
                            last = matmul_split(pe, p_q[:, i, :], [a[:, c, i * P:(i + 1) * P] for a in wq],
                                                [a[:, c, :] for a in x], c == 0, c == DC - 1)
                    t_q.mark(last)
                    if (t - 1).exists():
                        a_k.wait(pe, t - 1)
                    for i in range(DC):
                        for parity in range(2):
                            for c in range(DC):
                                last = matmul_split(
                                    pe, p_k[:, i, parity * D:(parity + 1) * D],
                                    [a[:, c, :].rearrange("p (k two) -> p two k", two=2)[:, parity, i * P:(i + 1) * P]
                                     for a in x],
                                    [a[:, c, :] for a in wk], c == 0, c == DC - 1)
                    t_k.mark(last)
                    if (t + 1).exists(last=count):
                        turn_h(t + 1)
                    if (t - 1).exists():
                        d_v.wait(pe, t - 1)
                    for v in range(NB):
                        for c in range(DC):
                            last = matmul_split(pe, p_v[:].rearrange("p c s -> p (c s)")[:, v * D:(v + 1) * D],
                                                [a[:, c, v * P:(v + 1) * P] for a in x],
                                                [a[:, c, :] for a in wv], c == 0, c == DC - 1)
                    t_v.mark(last)
                turns(pe, count, unroll, step)

            @block.scalar
            def _(act):
                def turned(t):
                    t_hT.wait(act, t)
                    if (t - 2).exists():
                        t_v.wait(act, t - 2)
                    a_hT.mark(act.copy(hT[t.step % 2][0][:], p_tr[:]))

                turned(first)

                def step(t):
                    for made, out, p, buf, stored in ((t_q, a_q, p_q, qT, s_q), (t_k, a_k, p_k, kT, s_k)):
                        made.wait(act, t)
                        if (t - 2).exists():
                            slot_wait(act, stored, t - 2)
                        out.mark(act.copy(buf[t.step % 2][:], p[:]))
                    if (t + 1).exists(last=count):
                        turned(t + 1)
                turns(act, count, unroll, step)

            @block.vector
            def _(dve):
                dve.memset(half[:], -0.5).then_inc(s_c, 1)

                def front(t):
                    slot_wait(dve, s_ld, t)
                    norm.statistics(dve, t)
                    if (t - 1).exists():
                        t_hT.wait(dve, t - 1)
                    norm.scale(dve, t, h)

                def turned(t):
                    a_hT.wait(dve, t)
                    x = hT[t.step % 2]
                    d_hT.mark(dve.tensor_tensor(x[1][:], p_tr[:], x[0][:].bitcast(F32), ALU.subtract))

                front(first)
                turned(first)

                def step(t):
                    if (t + 1).exists(last=count):
                        front(t + 1)
                        turned(t + 1)
                    t_v.wait(dve, t)
                    if (t - 2).exists():
                        slot_wait(dve, s_v, t - 2)
                    d_v.mark(dve.tensor_copy(vs[t.step % 2][:].rearrange("p v d -> p (v d)"),
                                             p_v[:].rearrange("p c s -> p (c s)")))
                turns(dve, count, unroll, step)


def attend_batch(nc, name, src, dst, scratch, w):
    with ExitStack() as ctx:
        m = Memory(nc, ctx, name)
        G, GB = 8, 2
        RING = 4
        AT = 6
        k_all = m.sbuf("k_all", NB, B, DC, P)
        v_all = m.sbuf("v_all", NB, B, D)
        q_blk = m.sbuf("q_blk", B, DC, P)
        at = [m.sbuf(f"at{j}", B, P) for j in range(AT)]
        mx, sm, rc, rt = (m.sbuf(k, P) for k in ("mx", "sm", "rc", "rt"))
        tri, fill, unseen = (m.sbuf(k, P) for k in ("tri", "fill", "unseen"))
        xt = [m.sbuf(f"xt{k}", GB, D) for k in range(2)]
        yt = [m.sbuf(f"yt{k}", GB, D) for k in range(2)]
        p_s = m.psum("p_s", B, P)
        p_o = [m.psum(f"p_o{k}", GB, D) for k in range(RING)]

        s_c, s_z = m.sem("s_c"), m.sem("s_z")
        s_k, s_v = ([m.sem(f"s_{n}{j}") for j in range(NB)] for n in "kv")
        s_q, (s_x, s_y) = m.sem("s_q"), ([m.sem(f"s_{n}{k}") for k in range(2)] for n in "xy")
        banks = [str(b) for b in range(4)]
        t_s, d_sub, a_e = (m.track(k, *banks) for k in ("t_s", "d_sub", "a_e"))
        d_mx, d_w = m.track("d_mx"), m.track("d_w", "sum", "rc", "mul")
        g_w = m.track("g_w")
        d_diag, g_diag = m.track("d_diag", "rt", "fill"), m.track("g_diag")
        t_o, d_y = m.track("t_o"), m.track("d_y")
        blocks = [(qb, jb) for qb in range(NB) for jb in range(qb + 1)]
        at_ = lambda n: Turn(n, 0, 1)
        last_of = [(qb + 1) * (qb + 2) // 2 - 1 for qb in range(NB)]
        HB = B // 2
        of_query = lambda qb: range(qb * (qb + 1) // 2, last_of[qb] + 1)

        def share(n):
            qb, jb = blocks[n]
            cuts = [(qb - 1) * G + G * k // (qb + 1) for k in range(qb + 2)]
            return range(cuts[jb], cuts[jb + 1]) if qb else ()

        last_groups = range((NB - 1) * G, NB * G)

        def rows_of(a, qb, g):
            return a.rearrange("(b s) d -> s b d", b=B)[qb * P:(qb + 1) * P, g * GB:(g + 1) * GB, :]

        with nc.Block() as block:
            @block.sync
            def _(sp):
                def load_q(qb):
                    sp.dma_start(q_blk[:].rearrange("p b c s -> p (b c) s"),
                                 scratch["q"].rearrange("p (a s) -> p a s", s=S)[:, :, qb * P:(qb + 1) * P]
                                 ).then_inc(s_q, 16)

                def load_k(jb):
                    sp.dma_start(k_all[:, jb].rearrange("p b c s -> p (b c) s"),
                                 scratch["k"].rearrange("p (a s) -> p a s", s=S)[:, :, jb * P:(jb + 1) * P]
                                 ).then_inc(s_k[jb], 16)

                def load_v(jb):
                    sp.dma_start(v_all[:, jb], scratch["v"].rearrange("p (b v d) -> p b v d", b=B, d=D)[:, :, jb, :]
                                 ).then_inc(s_v[jb], 16)

                def load_x(n):
                    sp.dma_start(xt[n % 2][:], rows_of(src, n // G, n % G)).then_inc(s_x[n % 2], 16)

                load_k(0)
                load_q(0)
                for t, k in ((tri, "tri"), (fill, "fill")):
                    sp.dma_start(t[:], w[k]).then_inc(s_c, 16)
                load_x(0)
                load_x(1)
                load_v(0)
                load_v(1)

                def put(n):
                    d_y.wait(sp, at_(n))
                    sp.dma_start(rows_of(dst, n // G, n % G), yt[n % 2][:]).then_inc(s_y[n % 2], 16)
                    if n + 2 < NB * G:
                        load_x(n + 2)

                for n, (qb, jb) in enumerate(blocks):
                    if jb == qb and qb + 1 < NB:
                        t_s.wait(sp, at_(n))
                        load_q(qb + 1)
                    if n == 0:
                        load_v(2)
                        load_v(3)
                        for j in range(1, NB):
                            load_k(j)
                    for g in share(n):
                        put(g)
                for g in last_groups:
                    put(g)
                for k in range(2):
                    sp.wait_ge(s_y[k], 16 * (NB * G // 2))

            @block.tensor
            def _(pe):
                pe.wait_ge(s_z, 1)

                def scores(n):
                    qb, jb = blocks[n]
                    if jb == 0:
                        pe.wait_ge(s_q, 16 * (qb + 1))
                    if jb == qb:
                        pe.wait_ge(s_k[jb], 16)
                    for b in range(B):
                        if b % 4 == 0 and n:
                            d_sub.wait(pe, at_(n - 1), str(b // 4))
                        for c in range(DC):
                            last = pe.matmul(p_s[:, b, :], k_all[:, jb, b, c, :], q_blk[:, b, c, :],
                                             start=c == 0, stop=c == DC - 1)
                        if b % 4 == 3:
                            t_s.mark(last, str(b // 4))

                def outputs(n):
                    qb = n // G
                    if n % G == 0:
                        d_w.wait(pe, at_(last_of[qb]), "mul")
                        g_w.wait(pe, at_(last_of[qb]))
                        d_diag.wait(pe, at_(qb), "fill")
                        g_diag.wait(pe, at_(qb))
                    if n == 0:
                        for jb in range(NB):
                            pe.wait_ge(s_v[jb], 16)
                    if n >= RING:
                        d_y.wait(pe, at_(n - RING))
                    for i in range(GB):
                        b = n % G * GB + i
                        for jb in range(NB):
                            lhs = at[of_query(qb)[jb] % AT][:, b, :] if jb <= qb else unseen[:]
                            last = pe.matmul(p_o[n % RING][:, i, :], lhs, v_all[:, jb, b, :],
                                             start=jb == 0, stop=jb == NB - 1)
                    t_o.mark(last)

                for n in range(len(blocks)):
                    scores(n)
                    for g in share(n):
                        outputs(g)
                for g in last_groups:
                    outputs(g)

            @block.scalar
            def _(act):
                for n, (qb, jb) in enumerate(blocks):
                    for k in range(4):
                        d_sub.wait(act, at_(n), str(k))
                        x = at[n % AT][:, 4 * k:4 * k + 4, :]
                        a_e.mark(act.activation(x, x, ACT.Exp, scale=D ** -0.5), str(k))

            @block.gpsimd
            def _(pool):
                pool.wait_ge(s_c, 32)
                for n, (qb, jb) in enumerate(blocks):
                    x, r = at[n % AT][:, HB:, :], rt if jb == qb else rc
                    d_w.wait(pool, at_(n), "rc")
                    if jb == qb:
                        d_diag.wait(pool, at_(qb), "rt")
                    g_w.mark(pool.tensor_tensor(x, x, r[:].unsqueeze(1).to_broadcast([P, HB, P]), ALU.mult))
                    if jb == qb:
                        g_w.wait(pool, at_(n))
                        g_diag.mark(pool.tensor_tensor(x, x, fill[:].unsqueeze(1).to_broadcast([P, HB, P]), ALU.add))

            @block.vector
            def _(dve):
                dve.memset(unseen[:], UNSEEN).then_inc(s_z, 1)
                dve.wait_ge(s_c, 32)

                def output(n):
                    t_o.wait(dve, at_(n))
                    dve.wait_ge(s_x[n % 2], 16 * (n // 2 + 1))
                    if n >= 2:
                        dve.wait_ge(s_y[n % 2], 16 * (n // 2))
                    d_y.mark(dve.tensor_tensor(yt[n % 2][:], p_o[n % RING][:], xt[n % 2][:], ALU.add))

                for n, (qb, jb) in enumerate(blocks):
                    t_s.wait(dve, at_(n))
                    if n:
                        d_sub.wait(dve, at_(n - 1))
                    d_mx.mark(dve.tensor_reduce(mx[:], p_s[:].rearrange("p b s -> p s b"), AX.X, ALU.max))
                    d_mx.wait(dve, at_(n))
                    if n >= AT:
                        t_o.wait(dve, at_((blocks[n - AT][0] + 1) * G - 1))
                    for k in range(4):
                        d_sub.mark(dve.tensor_tensor(at[n % AT][:, 4 * k:4 * k + 4, :], p_s[:, 4 * k:4 * k + 4, :],
                                                     mx[:].unsqueeze(1).to_broadcast([P, 4, P]), ALU.subtract), str(k))
                    a_e.wait(dve, at_(n))
                    if n:
                        d_w.wait(dve, at_(n - 1), "mul")
                        g_w.wait(dve, at_(n - 1))
                    x = at[n % AT][:].rearrange("p b s -> p s b")
                    d_w.mark(dve.tensor_reduce(sm[:], x, AX.X, ALU.add), "sum")
                    d_w.wait(dve, at_(n), "sum")
                    d_w.mark(dve.reciprocal(rc[:], sm[:]), "rc")
                    d_w.wait(dve, at_(n), "rc")
                    x, r = at[n % AT][:, 0:HB, :], rc
                    if jb == qb:
                        d_diag.mark(dve.tensor_tensor(rt[:], rc[:], tri[:], ALU.mult), "rt")
                        d_diag.wait(dve, at_(qb), "rt")
                        r = rt
                    d_w.mark(dve.tensor_tensor(x, x, r[:].unsqueeze(1).to_broadcast([P, HB, P]), ALU.mult), "mul")
                    if jb == qb:
                        d_w.wait(dve, at_(n), "mul")
                        d_diag.mark(dve.tensor_tensor(x, x, fill[:].unsqueeze(1).to_broadcast([P, HB, P]), ALU.add), "fill")
                    for g in share(n):
                        output(g)
                for g in last_groups:
                    output(g)


def clear_semaphores(nc):
    used = sorted(nc.released_uncleared_semaphores)
    assert set(range(used[0], used[-1] + 1)) <= set(nc.free_semaphores)
    with nc.Block() as block:
        @block.gpsimd
        def _(pool):
            pool.sem_clear(range(used[0], used[-1] + 1))


def macaron(nc, out, x, w):
    stages = [(expert_ffn, "f1"), (dilated_attention, "a1"), (expert_ffn, "f2"),
              (channel_mix, "c1"), (batch_attention, "b1"), (channel_mix, "c2")]
    src = x
    for n, (stage, name) in enumerate(stages):
        dst = out if n == len(stages) - 1 else nc.dram_tensor(f"x_{name}", (N, D), F32, kind="Internal").ap()
        stage(nc, name, src, dst, w)
        src = dst
        if n < len(stages) - 1:
            clear_semaphores(nc)


def layouts(i):
    turn = lambda a, *axes: np.ascontiguousarray(np.transpose(a, axes or None))
    heads = lambda a: turn(a.reshape(BR, 4, 4, HD), 0, 2, 3, 1)
    qkv, bias = i["L0_attn_Wqkv"][:BR], i["L0_attn_bqkv"][:BR]
    tri = np.triu(np.ones((P, P), np.float32))
    kone = np.zeros((P, 1), np.float32)
    kone[HD::SLOT] = 1
    slots = np.kron(np.eye(4, dtype=np.float32), np.ones((SLOT, 1), np.float32))
    return {
        "ident": np.eye(P, dtype=np.float32), "tri": tri, "fill": np.float32(UNSEEN) * (1 - tri), "kone": kone,
        "slots": slots,
        "wq": i["L0_ffn_W_q"], "up_embed": i["L0_ffn_up_embed"], "wdn": turn(i["L0_ffn_W_down"]),
        "keys": turn(i["L0_ffn_keys"], 2, 0, 3, 1).reshape(2 * HEADS, KEYS, KEYS),
        "wdown": turn(i["L0_ffn_down_embed"]), "wup": turn(i["L0_ffn_W_up"]),
        "aq": turn(qkv[:, :D], 0, 2, 1), "ak": turn(qkv[:, D:2 * D], 0, 2, 1), "av": turn(qkv[:, 2 * D:], 0, 2, 1),
        "abq": heads(bias[:, :D]), "abk": heads(bias[:, D:2 * D]), "abv": np.ascontiguousarray(bias[:, 2 * D:]),
        "ao": turn(i["L0_attn_Wout"][:BR], 0, 2, 1), "abo": np.ascontiguousarray(i["L0_attn_bout"][:BR]),
        "bq": turn(i["L1_attn_Wq"]), "bk": turn(i["L1_attn_Wk"]), "bv": turn(i["L1_attn_Wv"]),
        "wr": turn(i["L1_ffn_W_r"]), "wk": turn(i["L1_ffn_W_k"]), "wv": turn(i["L1_ffn_W_v"]),
        "mu_r": i["L1_ffn_mu_r"], "mu_k": i["L1_ffn_mu_k"],
    }


def kernel(**inputs):
    from concourse import bacc
    from concourse.bass_utils import run_bass_kernel_spmd

    inputs = {k: np.asarray(v) for k, v in inputs.items()}
    arrays = {"x": np.ascontiguousarray(inputs["L0_attn_x"]).reshape(N, D)}
    arrays.update({k: np.ascontiguousarray(v) for k, v in layouts(inputs).items()})
    nc = bacc.Bacc("TRN2", target_bir_lowering=False, num_devices=1)
    w = {k: nc.dram_tensor(k, a.shape, F32, kind="ExternalInput").ap() for k, a in arrays.items()}
    out = nc.dram_tensor("out", (N, D), F32, kind="ExternalOutput").ap()
    macaron(nc, out, w.pop("x"), w)
    result = run_bass_kernel_spmd(nc, [arrays], core_ids=[0])
    return result.results[0]["out"].reshape(B, S, D)
```
